# Optimizing a Trainium2 kernel written in Bass

```python
import numpy as np
import jax
import jax.numpy as jnp

def _softmax(x, axis=-1):
    return jax.nn.softmax(x, axis=axis)

def _gelu(x):
    return jax.nn.gelu(x, approximate=True)

def _silu(x):
    return jax.nn.silu(x)

def _sigmoid(x):
    return jax.nn.sigmoid(x)

def _layernorm(x, axis=-1, eps=1e-05):
    m = jnp.mean(x, axis=axis, keepdims=True)
    v = jnp.var(x, axis=axis, keepdims=True)
    return (x - m) / jnp.sqrt(v + eps)

def _scatter_add(tgt, idx, src, axis=0):
    return tgt.at[idx].add(src)

def _segment_sum(src, seg, n):
    return jax.ops.segment_sum(src, seg, n)
kernel_name = 'mk_hybrid_d1_jaxref_r8_4f498b'

def setup_inputs(seed: int=0):
    np.random.seed(seed)
    _w = jnp.asarray

    def _L0_attn_a_setup():
        import jax, jax.numpy as jnp
        import numpy as np
        B, T, C = (4, 256, 128)
        QH = 4
        D = C // QH
        EPS = 1e-05

        def _layernorm(x, g, b):
            mu = jnp.mean(x, axis=-1, keepdims=True)
            var = jnp.mean(jnp.square(x - mu), axis=-1, keepdims=True)
            return (x - mu) * jax.lax.rsqrt(var + EPS) * g + b
        key = jax.random.key(seed)
        k1, k2, k3 = jax.random.split(key, 3)
        residual = jax.random.normal(k1, (B, T, C), dtype=jnp.float32)
        w_fc = jax.random.normal(k2, (C, C), dtype=jnp.float32) * (1.0 / np.sqrt(C))
        w_proj = jax.random.normal(k3, (C, C), dtype=jnp.float32) * (1.0 / np.sqrt(C))
        ln_g = jnp.ones((C,), dtype=jnp.float32)
        ln_b = jnp.zeros((C,), dtype=jnp.float32)
        return {'residual': residual, 'w_fc': w_fc, 'w_proj': w_proj, 'ln_g': ln_g, 'ln_b': ln_b}
    _L0_attn_a_in = _L0_attn_a_setup()

    def _L0_attn_b_setup():
        import jax, jax.numpy as jnp
        import numpy as np
        B, S, H_HID, H = (4, 512, 128, 16)
        D = H_HID // H

        def _gated_deltanet(x, Wq, bq, Wk, bk, Wv, bv, Wbeta, bbeta, Wo, bo):
            batch, seq, _ = x.shape
            q = (x @ Wq + bq).reshape(batch, seq, H, D)
            k = (x @ Wk + bk).reshape(batch, seq, H, D)
            v = (x @ Wv + bv).reshape(batch, seq, H, D)
            k = k / (jnp.linalg.norm(k, axis=-1, keepdims=True) + 1e-06)
            beta = jax.nn.sigmoid(x @ Wbeta + bbeta)[..., None]
            q = jnp.transpose(q, (1, 0, 2, 3))
            k = jnp.transpose(k, (1, 0, 2, 3))
            v = jnp.transpose(v, (1, 0, 2, 3))
            beta = jnp.transpose(beta, (1, 0, 2, 3))

            def _step(Sm, inputs):
                q_t, k_t, v_t, beta_t = inputs
                Sk = jnp.einsum('bhde,bhe->bhd', Sm, k_t)
                delta = v_t - Sk
                Sm = Sm + beta_t[..., None] * jnp.einsum('bhd,bhe->bhde', delta, k_t)
                o_t = jnp.einsum('bhde,bhe->bhd', Sm, q_t)
                return (Sm, o_t)
            S0 = jnp.zeros((batch, H, D, D), dtype=x.dtype)
            _, outputs = jax.lax.scan(_step, S0, (q, k, v, beta))
            outputs = jnp.transpose(outputs, (1, 0, 2, 3)).reshape(batch, seq, H_HID)
            return outputs @ Wo + bo
        key = jax.random.key(seed)
        ks = jax.random.split(key, 12)
        sc = 1.0 / np.sqrt(H_HID)
        return {'x': jax.random.normal(ks[0], (B, S, H_HID), jnp.float32), 'Wq': jax.random.normal(ks[1], (H_HID, H_HID), jnp.float32) * sc, 'bq': jnp.zeros((H_HID,), jnp.float32), 'Wk': jax.random.normal(ks[2], (H_HID, H_HID), jnp.float32) * sc, 'bk': jnp.zeros((H_HID,), jnp.float32), 'Wv': jax.random.normal(ks[3], (H_HID, H_HID), jnp.float32) * sc, 'bv': jnp.zeros((H_HID,), jnp.float32), 'Wbeta': jax.random.normal(ks[4], (H_HID, H), jnp.float32) * sc, 'bbeta': jnp.zeros((H,), jnp.float32), 'Wo': jax.random.normal(ks[5], (H_HID, H_HID), jnp.float32) * sc, 'bo': jnp.zeros((H_HID,), jnp.float32)}
    _L0_attn_b_in = _L0_attn_b_setup()

    def _L0_ffn_setup():
        import jax, jax.numpy as jnp
        import numpy as np
        HIDDEN = 128
        NUM_EXPERTS = 8
        TOP_K = 2
        B, S = (2, 256)
        key = jax.random.key(seed)
        k1, k2, k3, k4, k5 = jax.random.split(key, 5)
        d, dff, E = (HIDDEN, 4 * HIDDEN, NUM_EXPERTS)
        x = jax.random.normal(k1, (B, S, d), dtype=jnp.float32)
        W1 = jax.random.normal(k2, (E, d, dff), dtype=jnp.float32) * (1.0 / np.sqrt(d))
        b1 = jax.random.normal(k3, (E, dff), dtype=jnp.float32) * 0.01
        W2 = jax.random.normal(k4, (E, dff, d), dtype=jnp.float32) * (1.0 / np.sqrt(dff))
        b2 = jax.random.normal(k5, (E, d), dtype=jnp.float32) * 0.01
        return {'x': x, 'W1': W1, 'b1': b1, 'W2': W2, 'b2': b2}
    _L0_ffn_in = _L0_ffn_setup()
    _d = {'L0_attn_a_residual': _L0_attn_a_in['residual'], 'L0_attn_a_w_fc': _L0_attn_a_in['w_fc'], 'L0_attn_a_w_proj': _L0_attn_a_in['w_proj'], 'L0_attn_a_ln_g': _L0_attn_a_in['ln_g'], 'L0_attn_a_ln_b': _L0_attn_a_in['ln_b'], 'L0_attn_b_Wq': _L0_attn_b_in['Wq'], 'L0_attn_b_bq': _L0_attn_b_in['bq'], 'L0_attn_b_Wk': _L0_attn_b_in['Wk'], 'L0_attn_b_bk': _L0_attn_b_in['bk'], 'L0_attn_b_Wv': _L0_attn_b_in['Wv'], 'L0_attn_b_bv': _L0_attn_b_in['bv'], 'L0_attn_b_Wbeta': _L0_attn_b_in['Wbeta'], 'L0_attn_b_bbeta': _L0_attn_b_in['bbeta'], 'L0_attn_b_Wo': _L0_attn_b_in['Wo'], 'L0_attn_b_bo': _L0_attn_b_in['bo'], 'L0_ffn_W1': _L0_ffn_in['W1'], 'L0_ffn_b1': _L0_ffn_in['b1'], 'L0_ffn_W2': _L0_ffn_in['W2'], 'L0_ffn_b2': _L0_ffn_in['b2']}
    _x0 = _d['L0_attn_a_residual']
    _d['L0_attn_a_residual'] = jax.random.normal(jax.random.fold_in(jax.random.key(seed), 1), (2, 1024, 128), dtype=_x0.dtype)
    del _x0
    return _d

def reference(L0_attn_a_residual, L0_attn_a_w_fc, L0_attn_a_w_proj, L0_attn_a_ln_g, L0_attn_a_ln_b, L0_attn_b_Wq, L0_attn_b_bq, L0_attn_b_Wk, L0_attn_b_bk, L0_attn_b_Wv, L0_attn_b_bv, L0_attn_b_Wbeta, L0_attn_b_bbeta, L0_attn_b_Wo, L0_attn_b_bo, L0_ffn_W1, L0_ffn_b1, L0_ffn_W2, L0_ffn_b2):

    def _L0_attn_a_ref(residual, w_fc, w_proj, ln_g, ln_b):
        import jax, jax.numpy as jnp
        import numpy as np
        B, T, C = (4, 256, 128)
        QH = 4
        D = C // QH
        EPS = 1e-05

        def _layernorm(x, g, b):
            mu = jnp.mean(x, axis=-1, keepdims=True)
            var = jnp.mean(jnp.square(x - mu), axis=-1, keepdims=True)
            return (x - mu) * jax.lax.rsqrt(var + EPS) * g + b
        Bx, Tx, Cx = residual.shape
        x = _layernorm(residual, ln_g, ln_b)
        q = x.reshape(Bx, Tx, QH, D).transpose(0, 2, 1, 3)
        k = w_fc.reshape(-1, D)
        v = w_proj.T.reshape(-1, D)
        scores = jnp.einsum('bhtd,sd->bhts', q, k)
        p = jnp.square(jax.nn.relu(scores))
        out = jnp.einsum('bhts,sd->bhtd', p, v)
        out = out.transpose(0, 2, 1, 3).reshape(Bx, Tx, Cx)
        return residual + out

    def _L0_attn_b_ref(x, Wq, bq, Wk, bk, Wv, bv, Wbeta, bbeta, Wo, bo):
        import jax, jax.numpy as jnp
        import numpy as np
        B, S, H_HID, H = (4, 512, 128, 16)
        D = H_HID // H

        def _gated_deltanet(x, Wq, bq, Wk, bk, Wv, bv, Wbeta, bbeta, Wo, bo):
            batch, seq, _ = x.shape
            q = (x @ Wq + bq).reshape(batch, seq, H, D)
            k = (x @ Wk + bk).reshape(batch, seq, H, D)
            v = (x @ Wv + bv).reshape(batch, seq, H, D)
            k = k / (jnp.linalg.norm(k, axis=-1, keepdims=True) + 1e-06)
            beta = jax.nn.sigmoid(x @ Wbeta + bbeta)[..., None]
            q = jnp.transpose(q, (1, 0, 2, 3))
            k = jnp.transpose(k, (1, 0, 2, 3))
            v = jnp.transpose(v, (1, 0, 2, 3))
            beta = jnp.transpose(beta, (1, 0, 2, 3))

            def _step(Sm, inputs):
                q_t, k_t, v_t, beta_t = inputs
                Sk = jnp.einsum('bhde,bhe->bhd', Sm, k_t)
                delta = v_t - Sk
                Sm = Sm + beta_t[..., None] * jnp.einsum('bhd,bhe->bhde', delta, k_t)
                o_t = jnp.einsum('bhde,bhe->bhd', Sm, q_t)
                return (Sm, o_t)
            S0 = jnp.zeros((batch, H, D, D), dtype=x.dtype)
            _, outputs = jax.lax.scan(_step, S0, (q, k, v, beta))
            outputs = jnp.transpose(outputs, (1, 0, 2, 3)).reshape(batch, seq, H_HID)
            return outputs @ Wo + bo
        return _gated_deltanet(x, Wq, bq, Wk, bk, Wv, bv, Wbeta, bbeta, Wo, bo)

    def _L0_ffn_ref(x, W1, b1, W2, b2):
        import jax, jax.numpy as jnp
        import numpy as np
        HIDDEN = 128
        NUM_EXPERTS = 8
        TOP_K = 2
        B, S = (2, 256)
        Bm, Sm, d = x.shape
        E = W1.shape[0]
        x_flat = x.reshape(-1, d)
        h = jnp.mod(x_flat[:, :TOP_K].sum(axis=1).astype(jnp.int32), E)
        sel = jnp.stack([h, jnp.mod(h + 1, E)], axis=1)

        def step(acc, params):
            e, W1e, b1e, W2e, b2e = params
            w = jnp.any(sel == e, axis=1).astype(x.dtype) / TOP_K
            y = jnp.maximum(x_flat @ W1e + b1e, 0.0) @ W2e + b2e
            return (acc + w[:, None] * y, None)
        init = jnp.zeros_like(x_flat)
        out_flat, _ = jax.lax.scan(step, init, (jnp.arange(E), W1, b1, W2, b2))
        return out_flat.reshape(Bm, Sm, d)
    x = L0_attn_a_residual
    x = x + _L0_attn_a_ref(_layernorm(x, axis=-1), L0_attn_a_w_fc, L0_attn_a_w_proj, L0_attn_a_ln_g, L0_attn_a_ln_b)
    x = x + _L0_ffn_ref(_layernorm(x, axis=-1), L0_ffn_W1, L0_ffn_b1, L0_ffn_W2, L0_ffn_b2)
    x = x + _L0_attn_b_ref(_layernorm(x, axis=-1), L0_attn_b_Wq, L0_attn_b_bq, L0_attn_b_Wk, L0_attn_b_bk, L0_attn_b_Wv, L0_attn_b_bv, L0_attn_b_Wbeta, L0_attn_b_bbeta, L0_attn_b_Wo, L0_attn_b_bo)
    x = x + _L0_ffn_ref(_layernorm(x, axis=-1), L0_ffn_W1, L0_ffn_b1, L0_ffn_W2, L0_ffn_b2)
    return x

_drawn_inputs = setup_inputs


def setup_inputs(seed=0):
    import zlib

    import numpy as np

    out = dict(_drawn_inputs(seed))
    spreads = {'L0_attn_a_ln_g': (1.0, 0.2),
     'L0_attn_a_ln_b': (0.0, 0.1),
     'L0_attn_b_bq': (0.0, 0.1),
     'L0_attn_b_bk': (0.0, 0.1),
     'L0_attn_b_bv': (0.0, 0.1),
     'L0_attn_b_bbeta': (0.0, 0.1),
     'L0_attn_b_bo': (0.0, 0.1)}
    factors = {'L0_ffn_b1': 8.0, 'L0_ffn_b2': 5.635}
    for name, (base, spread) in spreads.items():
        noise = np.random.default_rng([zlib.crc32(name.encode()), seed]).standard_normal(out[name].shape)
        drawn = base * np.exp(spread * noise) if base else spread * noise
        out[name] = jnp.asarray(drawn.astype(out[name].dtype))
    for name, factor in factors.items():
        out[name] = (out[name] * factor).astype(out[name].dtype)
    return out
```

```python
from contextlib import ExitStack

import concourse.bass as bass
from concourse import mybir

ALU = mybir.AluOpType
ACT = mybir.ActivationFunctionType
F32 = mybir.dt.float32
AX_X = mybir.AxisListType.X

P = 128
C = 128
NB = 2
BLK = 8
QT_ = 4
NQ = NB * BLK // QT_
NE = 8
FF = 512
FC = FF // P
AH = 4
AD = C // AH
NM = 4
H = 16
D = C // H
R = 2 * D
PW = 3 * C + H
SEG = 32
EPS = 1e-5
ROUND = 2.0 ** 23
ROUND_S = 1.5 * 2.0 ** 23


def attention(q):
    s = [("stats", "Y", q), ("norm", "Y", q), ("stats", "Z", q), ("norm", "Z", q), ("turn", "x", "Z", q)]
    for h in range(AH):
        s.append(("score", q, h))
        if h:
            s.append(("mix", q, h - 1))
    return s + [("mix", q, AH - 1), ("mixed", q)]


def route(f):
    return [("stats", "F", f), ("norm", "F", f), ("route", f), ("turn", "x", "F", f), ("turn", "w", f),
            ("bias2", f), ("bias2ed", f)]


def experts(fs, more):
    units = [(f, e) for f in fs for e in range(NE)]
    s = []
    for u in range(len(units) + 1):
        own = []
        if u < len(units):
            own += [("up", *units[u], c) for c in range(FC)]
        if u:
            own += [("down", *units[u - 1], i) for i in range(QT_)] + [("weigh", *units[u - 1])]
        other = more.get(u, [])
        done = 0
        for n, stage in enumerate(own):
            s.append(stage)
            upto = len(other) * (n + 1) // len(own)
            s += other[done:upto]
            done = upto
    return s


def project(b):
    s = []
    for q in (2 * b, 2 * b + 1):
        s += [("stats", "D", q), ("norm", "D", q), ("turn", "x", "D", q)]
    return s + [("project", b, j) for j in range(BLK)] + [("keys", b)]


def transfers(b):
    return ([("turn", "P", b, n) for n in range(2)] + [("turn", "Q", b, n) for n in range(2)]
            + [("unfold", b, n) for n in range(2)])


def chain(b):
    return [("state", b, g) for g in range(P - 1)]


def read_out(b):
    s = [("turn", "S", b, n) for n in range(2)] + [("read", b, j) for j in range(BLK)]
    for n in range(2):
        s += [("turn", "O", b, n), ("out", b, n), ("outed", b, n)]
    return s


def plan():
    m0 = [("block", 0, j) for j in range(BLK)]
    m1 = [("block", 1, j) for j in range(BLK)]
    s = attention(0) + attention(1) + route(0) + route(1) + experts((0, 1), {})
    s += attention(2) + attention(3) + route(2) + route(3) + project(0)
    s += experts((2, 3), {2 * j: [m0[j]] for j in range(BLK)})
    s += project(1) + transfers(0) + m1[:3] + chain(0) + read_out(0) + route(4) + route(5)
    c1 = chain(1)
    more = {u: [m1[3 + u]] for u in range(5)}
    more[6] = transfers(1)
    for u in range(7, 17):
        more[u] = c1[8 * (u - 7):8 * (u - 6)]
    s += experts((4, 5), more) + c1[80:]
    s += read_out(1) + route(6) + route(7) + experts((6, 7), {})
    return s


def layer_kernel(nc, residual, w_fc, w_proj, ln_g, ln_b, Wq, bq, Wk, bk, Wv, bv, Wbeta, bbeta, Wo, bo,
                 W1, b1, W2, b2, out):
    stages = plan()

    def order(*kinds):
        return {s: n for n, s in enumerate(x for x in stages if x[0] in kinds)}

    norm_no = order("norm")
    turn_no = order("turn")
    turns = 2 + len(turn_no)
    score_no = order("score")
    up_no = order("up")
    y_no = {}
    for s in stages:
        if s[0] == "mix" and s[2] == 0:
            y_no["mix", s[1]] = len(y_no)
        elif s[0] in ("bias2", "project", "out"):
            y_no[s] = len(y_no)
        elif s[0] == "down" and s[3] == 0:
            y_no["down", s[1], s[2]] = len(y_no)
    z_no, z = {}, 0
    for s in stages:
        if s[0] == "score":
            z_no[s] = z
            z += 2
        elif s[0] == "up":
            z_no[s] = z
            z += 1
    block_no, state_no, unfold_no, read_no = order("block"), order("state"), order("unfold"), order("read")
    out_no = order("out")

    with ExitStack() as ctx:
        def sb(name, shape):
            return ctx.enter_context(nc.sbuf_tensor(name, [P, *shape], F32))

        def bank(name):
            return ctx.enter_context(nc.psum_tensor(name, [P, 512], F32))

        def sem(name):
            return ctx.enter_context(nc.semaphore(name))

        X = sb("X", [NB * BLK, C])
        w1 = sb("w1", [NE, FF])
        w2 = sb("w2", [NE, FC, C])
        b1_rows = sb("b1_rows", [P])
        b1_cols = sb("b1_cols", [NE * FC])
        b2_rows = sb("b2_rows", [C])
        wfc = sb("wfc", [C])
        wproj = sb("wproj", [C])
        wfc4 = sb("wfc4", [NM, AH, AD])
        table_k = sb("table_k", [NM, AH, P])
        table_v = sb("table_v", [NM, AD])
        gain = sb("gain", [1])
        shift = sb("shift", [1])
        w_in = sb("w_in", [PW])
        b_in = sb("b_in", [PW])
        w_out = sb("w_out", [C])
        b_out = sb("b_out", [C])
        ones = sb("ones", [P])
        ident = sb("ident", [P])
        numbers = sb("numbers", [NE])
        halves = sb("halves", [2 * P])
        stat = sb("stat", [2, QT_, 6])
        mv = sb("mv", [2, QT_, 2])
        var_eps = sb("var_eps", [2, QT_])
        rstd = sb("rstd", [2, QT_])
        YN = sb("YN", [4, QT_, C])
        zT = sb("zT", [2, QT_ * P])
        xT = sb("xT", [4, QT_ * P])
        rt = sb("rt", [8, QT_])
        hit = sb("hit", [QT_, NE])
        wt = sb("wt", [4, QT_, NE])
        wT = sb("wT", [2, QT_ * P])
        hid = sb("hid", [2, 4, 512])
        qkvb = sb("qkvb", [BLK, PW])
        nkb = sb("nkb", [BLK, C])
        beta = sb("beta", [BLK, H])
        kn = sb("kn", [3, BLK, H])
        M = sb("M", [R, H, D])
        tmp = sb("tmp", [R, H, D])
        dl = sb("dl", [R, H])
        res = sb("res", [NB, BLK, R, H])
        pT = sb("pT", [D, P])
        qT = sb("qT", [D, P])
        unfolded = sb("unfolded", [2, H, D, SEG])
        ST = sb("ST", [D, P])
        S = sb("S", [D, H, D])
        O = sb("O", [BLK, H, D])
        oT = sb("oT", [BLK, P])

        TB = [bank(f"TB{i}") for i in range(2)]
        ZB = [bank(f"ZB{i}") for i in range(2)]
        YB = [bank(f"YB{i}") for i in range(2)]
        CB = [bank(f"CB{i}") for i in range(2)]

        x_in = [sem(f"x_in{q}") for q in range(NQ)]
        consts_in = sem("consts_in")
        w_in_in = sem("w_in_in")
        ff_in = sem("ff_in")
        pool_consts = sem("pool_consts")
        ident_ready = sem("ident_ready")
        var_ready = sem("var_ready")
        eps_added = sem("eps_added")
        rstd_ready = sem("rstd_ready")
        norm_ready = sem("norm_ready")
        wfc4_ready = sem("wfc4_ready")
        turn_full = sem("turn_full")
        turn_used = sem("turn_used")
        z_full = sem("z_full")
        z_used = sem("z_used")
        square_act = sem("square_act")
        c_full = sem("c_full")
        relu_dve = sem("relu_dve")
        square_pool = sem("square_pool")
        y_full = sem("y_full")
        y_used = sem("y_used")
        route_ready = sem("route_ready")
        beta_ready = sem("beta_ready")
        length2_ready = sem("length2_ready")
        length_ready = sem("length_ready")
        blocks_done = sem("blocks_done")
        unfold_zeroed = sem("unfold_zeroed")
        unfold_in = [sem(f"unfold_in{i}") for i in range(2)]
        state_full = sem("state_full")
        state_ready = sem("state_ready")
        o_ready = sem("o_ready")
        stored = sem("stored")
        dve_done = sem("dve_done")

        N_SMALL = 7

        def quad(t, q):
            return t[:, q * QT_:(q + 1) * QT_, :]

        def flat(ap):
            return ap.rearrange("p a b -> p (a b)")

        def x_dram(t, q):
            b, half = divmod(q, 2)
            return t[b].rearrange("(g j) c -> g j c", j=BLK)[:, half * QT_:(half + 1) * QT_, :]

        def turned(s):
            return 2 + turn_no[s] + 1

        block = ctx.enter_context(nc.Block())

        @block.sync
        def _(sp):
            sp.dma_start(quad(X, 0), x_dram(residual, 0)).then_inc(x_in[0], 16)
            sp.dma_start(wfc[:, :], w_fc).then_inc(consts_in, 16)
            sp.dma_start(wproj[:, :], w_proj).then_inc(consts_in, 16)
            sp.dma_start(gain[:, :], ln_g.rearrange("(c o) -> c o", o=1)).then_inc(consts_in, 16)
            sp.dma_start(shift[:, :], ln_b.rearrange("(c o) -> c o", o=1)).then_inc(consts_in, 16)
            sp.dma_start(b1_rows[0:NE * FC, :], b1.rearrange("e (c p) -> (e c) p", p=P)).then_inc(consts_in, 16)
            sp.dma_start(b2_rows[0:NE, :], b2).then_inc(consts_in, 16)
            sp.dma_start(b_out[0:1, :], bo.rearrange("(o c) -> o c", o=1)).then_inc(consts_in, 16)
            for q in range(1, NQ):
                sp.dma_start(quad(X, q), x_dram(residual, q)).then_inc(x_in[q], 16)
            for e in range(NE):
                sp.dma_start(w1[:, e, :], W1[e]).then_inc(ff_in, 16)
                sp.dma_start(w2[:, e, :, :], W2[e].rearrange("(c p) d -> p c d", p=P)).then_inc(ff_in, 16)
            at = 0
            for w, bias in ((Wq, bq), (Wk, bk), (Wv, bv), (Wbeta, bbeta)):
                n = w.shape[1]
                sp.dma_start(w_in[:, at:at + n], w).then_inc(w_in_in, 16)
                sp.dma_start(b_in[:, at:at + n],
                             bias.rearrange("(o c) -> o c", o=1).broadcast_to([P, n])).then_inc(w_in_in, 16)
                at += n
            sp.dma_start(w_out[:, :], Wo).then_inc(w_in_in, 16)

            def unfold(b, seg):
                n = b * (P // SEG) + seg
                if seg >= 2:
                    sp.wait_ge(state_full, state_no["state", b, (seg - 1) * SEG - 1] + 1)
                sp.wait_ge(turn_used, turned(("turn", "P", b, 1)))
                for h in range(H):
                    sp.dma_start(unfolded[h * D:(h + 1) * D, n % 2, h, :, :],
                                 pT[h:P:H, :, seg * SEG:(seg + 1) * SEG]).then_inc(unfold_in[n % 2], 16)

            sp.wait_ge(unfold_zeroed, 1)
            for s in stages:
                if s[0] == "unfold":
                    unfold(s[1], s[2])
                elif s[0] == "state" and s[2] in (SEG, 2 * SEG):
                    unfold(s[1], s[2] // SEG + 1)
            for q in range(NQ):
                sp.wait_ge(y_used, y_no["down", NQ + q, NE - 1] + 1)
                sp.dma_start(x_dram(out, q), quad(X, q)).then_inc(stored, 16)
            sp.wait_ge(stored, 16 * NQ)

        @block.gpsimd
        def _(pool):
            pool.memset(ident[:, :], 1.0).then_inc(pool_consts, 1)
            pool.wait_ge(pool_consts, 1)
            pool.affine_select(out=ident[:, :], in_=ident[:, :], compare_op=ALU.is_equal, fill=0.0, base=0,
                               pattern=[[-1, P]], channel_multiplier=1).then_inc(ident_ready, 1)
            pool.memset(halves[:, 0:P], -0.5)
            pool.memset(halves[:, P:2 * P], 0.5).then_inc(pool_consts, 1)
            pool.wait_ge(pool_consts, 2)
            pool.memset(table_k[:, :, :, :], 0.0)
            pool.memset(ones[:, :], 1.0)
            pool.iota(numbers[:, :], pattern=[[1, NE]], base=0, channel_multiplier=0,
                      allow_small_or_imprecise_dtypes=True)
            pool.memset(ST[:, :, 0:1], 0.0).then_inc(pool_consts, 1)
            unfold_set = False
            for s in stages:
                if s[0] == "stats":
                    n = norm_no["norm", s[1], s[2]]
                    pool.wait_ge(var_ready, n + 1)
                    pool.tensor_scalar(var_eps[:, n % 2, :], mv[:, n % 2, :, 1], EPS, 1.0, ALU.add,
                                       ALU.mult).then_inc(eps_added, 1)
                    pool.wait_ge(eps_added, n + 1)
                    pool.tensor_tensor(rstd[:, n % 2, :], var_eps[:, n % 2, :], halves[:, 0:QT_],
                                       ALU.pow).then_inc(rstd_ready, 1)
                elif s[0] == "score":
                    n = score_no[s]
                    for m in (2, 3):
                        pool.wait_ge(relu_dve, 2 * n + m - 1)
                        pool.tensor_tensor(hid[:, n % 2, m, :], hid[:, n % 2, m, :], hid[:, n % 2, m, :],
                                           ALU.mult).then_inc(square_pool, 1)
                elif s[0] == "keys":
                    pool.wait_ge(length2_ready, s[1] + 1)
                    pool.tensor_tensor(flat(kn[:, 1, :, :]), flat(kn[:, 0, :, :]), halves[:, P:2 * P],
                                       ALU.pow).then_inc(length_ready, 1)
                if not unfold_set and s[0] == "up":
                    unfold_set = True
                    pool.memset(unfolded[:, :, :, :, :], 0.0).then_inc(unfold_zeroed, 1)

        @block.tensor
        def _(pe):
            fills = [0]

            def turn(parts, n):
                bank_ = TB[n % 2]
                if n >= 2:
                    pe.wait_ge(turn_used, n - 1)
                for at, ap, rows, cols in parts:
                    last = pe.transpose(bank_[0:rows, at:at + cols], ap, ident[0:cols, 0:cols])
                last.then_inc(turn_full, 1)

            def y_bank(key):
                n = y_no[key]
                if n >= 2:
                    pe.wait_ge(y_used, n - 1)
                return YB[n % 2]

            pe.wait_ge(ident_ready, 1)
            pe.wait_ge(consts_in, 16 * N_SMALL)
            pe.wait_ge(wfc4_ready, 1)
            turn([(m * P, flat(wfc4[:, m, :, :]), P, P) for m in range(NM)], 0)
            turn([(0, wproj[:, :], P, P), (P, b1_rows[0:NE * FC, :], P, NE * FC)], 1)
            pe.wait_ge(pool_consts, 3)
            unfolds = 0
            for s in stages:
                kind = s[0]
                if kind == "turn":
                    n = 2 + turn_no[s]
                    what = s[1]
                    if what == "x":
                        k = norm_no["norm", s[2], s[3]]
                        pe.wait_ge(norm_ready, k + 1)
                        turn([(i * P, YN[:, k % 4, i, :], P, P) for i in range(QT_)], n)
                    elif what == "w":
                        pe.wait_ge(route_ready, s[2] + 1)
                        turn([(i * P, wt[:, s[2] % 4, i, :], NE, P) for i in range(QT_)], n)
                    elif what == "P":
                        pe.wait_ge(blocks_done, s[2] + 1)
                        turn([(i * P, flat(M[:, D:R, :, 4 * s[3] + i]), P, P) for i in range(4)], n)
                    elif what == "Q":
                        pe.wait_ge(blocks_done, s[2] + 1)
                        turn([(i * P, flat(M[:, 4 * s[3] + i, :, :]), P, P) for i in range(4)], n)
                    elif what == "S":
                        pe.wait_ge(state_ready, state_no["state", s[2], P - 2] + 1)
                        turn([(i * P, ST[:, 4 * s[3] + i, :], P, P) for i in range(4)], n)
                    elif what == "O":
                        pe.wait_ge(o_ready, read_no["read", s[2], 4 * s[3] + 3] + 1)
                        turn([(i * P, O[:, 4 * s[3] + i, :, :].rearrange("p h d -> p (h d)"), P, P)
                              for i in range(4)], n)
                elif kind == "score":
                    q, h = s[1:]
                    pe.wait_ge(turn_used, turned(("turn", "x", "Z", q)))
                    k = score_no[s]
                    for m in range(NM):
                        if m < 2:
                            z = z_no[s] + m
                            if z >= 2:
                                pe.wait_ge(z_used, z - 1)
                            to, full = ZB[z % 2], z_full
                        else:
                            if k >= 1:
                                pe.wait_ge(relu_dve, 2 * (k - 1) + m - 1)
                            to, full = CB[m - 2], c_full
                        pe.matmul(to[:, :], table_k[:, m, h, :], zT[:, q % 2, :], start=True,
                                  stop=True).then_inc(full, 1)
                elif kind == "mix":
                    q, h = s[1:]
                    k = score_no["score", q, h]
                    if h == 0:
                        y_bank(("mix", q))
                    yb = YB[y_no["mix", q] % 2]
                    pe.wait_ge(square_act, 2 * (k + 1))
                    pe.wait_ge(square_pool, 2 * (k + 1))
                    for i in range(QT_):
                        for m in range(NM):
                            last = pe.matmul(yb[:, i * C + h * AD:i * C + (h + 1) * AD],
                                             hid[:, k % 2, m, i * P:(i + 1) * P], table_v[:, m, :],
                                             start=(m == 0), stop=(m == NM - 1))
                    if h == AH - 1:
                        last.then_inc(y_full, 1)
                elif kind == "bias2":
                    f = s[1]
                    pe.wait_ge(turn_used, turned(("turn", "w", f)))
                    yb = y_bank(s)
                    for i in range(QT_):
                        last = pe.matmul(yb[:, i * C:(i + 1) * C], wT[0:NE, f % 2, i * P:(i + 1) * P],
                                         b2_rows[0:NE, :], start=True, stop=True)
                    last.then_inc(y_full, 1)
                elif kind == "up":
                    f, e, c = s[1:]
                    if e == 0 and c == 0:
                        pe.wait_ge(ff_in, 16 * 2 * NE)
                        pe.wait_ge(turn_used, turned(("turn", "x", "F", f)))
                    z = z_no[s]
                    if z >= 2:
                        pe.wait_ge(z_used, z - 1)
                    pe.matmul(ZB[z % 2][:, :], w1[:, e, c * P:(c + 1) * P], xT[:, f % 4, :], start=True,
                              stop=True).then_inc(z_full, 1)
                elif kind == "down":
                    f, e, i = s[1:]
                    u = f * NE + e
                    if i == 0:
                        y_bank(("down", f, e))
                        pe.wait_ge(z_used, z_no["up", f, e, FC - 1] + 1)
                    yb = YB[y_no["down", f, e] % 2]
                    for c in range(FC):
                        last = pe.matmul(yb[:, i * C:(i + 1) * C], hid[:, u % 2, c, i * P:(i + 1) * P],
                                         w2[:, e, c, :], start=(c == 0), stop=(c == FC - 1))
                    if i == QT_ - 1:
                        last.then_inc(y_full, 1)
                elif kind == "project":
                    b, j = s[1:]
                    if j == 0:
                        pe.wait_ge(w_in_in, 16 * 9)
                    pe.wait_ge(turn_used, turned(("turn", "x", "D", 2 * b + j // QT_)))
                    i = j % QT_
                    pe.matmul(y_bank(s)[:, 0:PW], zT[:, j // QT_, i * P:(i + 1) * P], w_in[:, :], start=True,
                              stop=True).then_inc(y_full, 1)
                elif kind == "state":
                    b, g = s[1:]
                    seg = b * (P // SEG) + g // SEG
                    if g == 0:
                        pe.wait_ge(turn_used, turned(("turn", "Q", b, 1)))
                    to = CB[g % 2][:, 0:D]
                    k = state_no[s]
                    if k >= 2:
                        pe.wait_ge(state_ready, k - 1)
                    if g % SEG == 0:
                        pe.wait_ge(unfold_in[seg % 2], 16 * H * (seg // 2 + 1))
                    pe.matmul(to, ident[:, :], qT[:, :, g], start=True, stop=False)
                    if k >= 1:
                        pe.wait_ge(state_ready, k)
                    pe.matmul(to, unfolded[:, seg % 2, :, :, g % SEG].rearrange("p h e -> p (h e)"),
                              ST[:, :, g], start=False, stop=True).then_inc(state_full, 1)
                elif kind == "out":
                    b, n = s[1:]
                    pe.wait_ge(turn_used, turned(("turn", "O", b, n)))
                    yb = y_bank(s)
                    for i in range(QT_):
                        pe.matmul(yb[:, i * C:(i + 1) * C], ones[0:1, :], b_out[0:1, :], start=True, stop=False)
                        last = pe.matmul(yb[:, i * C:(i + 1) * C], oT[:, n * QT_ + i, :], w_out[:, :],
                                         start=False, stop=True)
                    last.then_inc(y_full, 1)

        @block.scalar
        def _(act):
            act.wait_ge(pool_consts, 3)
            act.wait_ge(turn_full, 1)
            for h in range(AH):
                rows = slice(h * AD, (h + 1) * AD)
                last = act.activation(table_k[rows, :, h, :], TB[0][rows, :].rearrange("p (m c) -> p m c", m=NM),
                                      ACT.Copy)
            last.then_inc(turn_used, 1)
            act.wait_ge(turn_full, 2)
            act.activation(table_v[:, :, :], TB[1][:, 0:C].rearrange("p (m d) -> p m d", m=NM), ACT.Copy)
            act.activation(b1_cols[:, :], TB[1][:, P:P + NE * FC], ACT.Copy).then_inc(turn_used, 1)
            for s in stages:
                kind = s[0]
                if kind == "turn":
                    n = 2 + turn_no[s]
                    act.wait_ge(turn_full, n + 1)
                    tb = TB[n % 2]
                    four = tb[:, :].rearrange("p (i t) -> p i t", i=4)
                    what = s[1]
                    if what == "x" and s[2] == "Z":
                        act.wait_ge(consts_in, 16 * N_SMALL)
                        ins = act.activation(zT[:, s[3] % 2, :], tb[:, :], ACT.Identity, bias=shift[:, 0:1],
                                             scale=gain[:, 0:1])
                    elif what == "x" and s[2] == "F":
                        ins = act.activation(xT[:, s[3] % 4, :], tb[:, :], ACT.Copy)
                    elif what == "x":
                        ins = act.activation(zT[:, s[3] % 2, :], tb[:, :], ACT.Copy)
                    elif what == "w":
                        ins = act.activation(wT[0:NE, s[2] % 2, :], tb[0:NE, :], ACT.Copy)
                    elif what == "P":
                        ins = act.activation(pT[:, 4 * s[3]:4 * s[3] + 4, :], four, ACT.Copy)
                    elif what == "Q":
                        ins = act.activation(qT[:, 4 * s[3]:4 * s[3] + 4, :], four, ACT.Copy)
                    elif what == "S":
                        ins = act.activation(S[:, 4 * s[3]:4 * s[3] + 4, :, :],
                                             tb[:, :].rearrange("p (d h e) -> p d h e", d=4, h=H), ACT.Copy)
                    elif what == "O":
                        ins = act.activation(oT[:, 4 * s[3]:4 * s[3] + 4, :], four, ACT.Copy)
                    ins.then_inc(turn_used, 1)
                elif kind == "score":
                    k = score_no[s]
                    for m in range(2):
                        z = z_no[s] + m
                        act.wait_ge(z_full, z + 1)
                        act.activation(hid[:, k % 2, m, :], ZB[z % 2][:, :], ACT.Relu).then_inc(z_used, 1)
                        act.wait_ge(z_used, z + 1)
                        act.activation(hid[:, k % 2, m, :], hid[:, k % 2, m, :], ACT.Square)\
                           .then_inc(square_act, 1)
                elif kind == "up":
                    f, e, c = s[1:]
                    u = f * NE + e
                    z = z_no[s]
                    act.wait_ge(z_full, z + 1)
                    n = e * FC + c
                    act.activation(hid[:, u % 2, c, :], ZB[z % 2][:, :], ACT.Relu,
                                   bias=b1_cols[:, n:n + 1]).then_inc(z_used, 1)
                elif kind == "keys":
                    act.wait_ge(y_used, y_no["project", s[1], BLK - 1] + 1)
                    act.activation(beta[:, :, :], qkvb[:, :, 3 * C:PW], ACT.Sigmoid).then_inc(beta_ready, 1)
                elif kind == "state":
                    b, g = s[1:]
                    act.wait_ge(state_full, state_no[s] + 1)
                    act.activation(ST[:, :, g + 1], CB[g % 2][:, 0:D], ACT.Copy).then_inc(state_ready, 1)

        @block.vector
        def _(dve):
            links = [0]

            def link(ins):
                links[0] += 1
                ins.then_inc(dve_done, 1)
                dve.wait_ge(dve_done, links[0])

            dve.wait_ge(consts_in, 16 * N_SMALL)
            for m in range(NM):
                last = dve.tensor_copy(wfc4[:, m, :, :], wfc[:, m * AD:(m + 1) * AD]
                                       .rearrange("p (o d) -> p o d", o=1).to_broadcast([P, AH, AD]))
            last.then_inc(wfc4_ready, 1)
            dve.wait_ge(pool_consts, 3)
            for s in stages:
                kind = s[0]
                if kind == "stats":
                    what, q = s[1:]
                    n = norm_no["norm", what, q]
                    if what == "Y":
                        dve.wait_ge(x_in[q], 16)
                    src = YN[:, norm_no["norm", "Y", q] % 4, :, :] if what == "Z" else quad(X, q % NQ)
                    for i in range(QT_):
                        last = dve.bn_stats(stat[:, n % 2, i, :], src[:, i, :])
                    link(last)
                    for i in range(QT_):
                        last = dve.bn_aggr(mv[:, n % 2, i, :], stat[:, n % 2, i, :])
                    last.then_inc(var_ready, 1)
                elif kind == "norm":
                    what, q = s[1:]
                    n = norm_no[s]
                    src = YN[:, norm_no["norm", "Y", q] % 4, :, :] if what == "Z" else quad(X, q % NQ)
                    dve.wait_ge(rstd_ready, n + 1)
                    old = [t for t in turn_no if t[1] == "x" and norm_no["norm", t[2], t[3]] == n - 4]
                    if old:
                        dve.wait_ge(turn_full, 2 + turn_no[old[0]] + 1)
                    for i in range(QT_):
                        last = dve.tensor_scalar(YN[:, n % 4, i, :], src[:, i, :], mv[:, n % 2, i, 0:1],
                                                 rstd[:, n % 2, i:i + 1], ALU.subtract, ALU.mult)
                    last.then_inc(norm_ready, 1)
                    dve.wait_ge(norm_ready, n + 1)
                    if what == "Y":
                        link(dve.tensor_tensor(flat(quad(X, q)), flat(quad(X, q)), flat(YN[:, n % 4, :, :]),
                                               ALU.add))
                elif kind == "score":
                    k = score_no[s]
                    for m in (2, 3):
                        dve.wait_ge(c_full, 2 * k + m - 1)
                        dve.tensor_scalar(hid[:, k % 2, m, :], CB[m - 2][:, :], 0.0, None, ALU.max)\
                           .then_inc(relu_dve, 1)
                elif kind in ("mixed", "bias2ed", "outed"):
                    if kind == "mixed":
                        y, q = y_no["mix", s[1]], s[1]
                    elif kind == "bias2ed":
                        y, q = y_no["bias2", s[1]], s[1] % NQ
                    else:
                        y, q = y_no["out", s[1], s[2]], 2 * s[1] + s[2]
                    dve.wait_ge(y_full, y + 1)
                    link_to = dve.tensor_tensor(flat(quad(X, q)), flat(quad(X, q)), YB[y % 2][:, :], ALU.add)
                    link_to.then_inc(y_used, 1)
                    dve.wait_ge(y_used, y + 1)
                elif kind == "route":
                    f = s[1]
                    y = YN[:, norm_no["norm", "F", f] % 4, :, :]
                    sm, ab, rd, up_, fl, ng, t8, hh = (rt[:, i, :] for i in range(8))
                    link(dve.tensor_tensor(sm, y[:, :, 0], y[:, :, 1], ALU.add))
                    link(dve.scalar_tensor_tensor(out=ab, in0=sm, scalar=-1.0, in1=sm, op0=ALU.mult, op1=ALU.max))
                    link(dve.tensor_scalar(rd, ab, ROUND, None, ALU.add))
                    link(dve.tensor_scalar(rd, rd, ROUND, None, ALU.subtract))
                    link(dve.tensor_tensor(up_, rd, ab, ALU.is_gt))
                    link(dve.tensor_tensor(fl, rd, up_, ALU.subtract))
                    link(dve.tensor_scalar(ng, sm, 0.0, -2.0, ALU.is_lt, ALU.mult))
                    link(dve.scalar_tensor_tensor(out=hh, in0=ng, scalar=1.0, in1=fl, op0=ALU.add, op1=ALU.mult))
                    link(dve.tensor_scalar(t8, hh, 1.0 / NE, None, ALU.mult))
                    link(dve.tensor_scalar(rd, t8, ROUND_S, None, ALU.add))
                    link(dve.tensor_scalar(rd, rd, ROUND_S, None, ALU.subtract))
                    link(dve.tensor_tensor(up_, rd, t8, ALU.is_gt))
                    link(dve.tensor_tensor(fl, rd, up_, ALU.subtract))
                    link(dve.scalar_tensor_tensor(out=hh, in0=fl, scalar=-float(NE), in1=hh, op0=ALU.mult,
                                                  op1=ALU.add))
                    link(dve.tensor_tensor(hit[:, :, :],
                                           hh.rearrange("p (i o) -> p i o", o=1).to_broadcast([P, QT_, NE]),
                                           numbers[:, :].rearrange("p (o e) -> p o e", o=1)
                                           .to_broadcast([P, QT_, NE]), ALU.is_equal))
                    w = wt[:, f % 4, :, :]
                    link(dve.tensor_scalar(hit[:, :, :], hit[:, :, :], 0.5, None, ALU.mult))
                    if f >= 4:
                        dve.wait_ge(turn_full, 2 + turn_no["turn", "w", f - 4] + 1)
                    dve.tensor_tensor(w[:, :, 1:NE], hit[:, :, 1:NE], hit[:, :, 0:NE - 1], ALU.add)
                    dve.tensor_tensor(w[:, :, 0:1], hit[:, :, 0:1], hit[:, :, NE - 1:NE], ALU.add)\
                       .then_inc(route_ready, 1)
                    dve.wait_ge(route_ready, f + 1)
                elif kind == "weigh":
                    f, e = s[1:]
                    y = y_no["down", f, e]
                    dve.wait_ge(y_full, y + 1)
                    for i in range(QT_):
                        xq = X[:, (f % NQ) * QT_ + i, :]
                        last = dve.scalar_tensor_tensor(out=xq, in0=YB[y % 2][:, i * C:(i + 1) * C],
                                                        scalar=wt[:, f % 4, i, e:e + 1], in1=xq, op0=ALU.mult,
                                                        op1=ALU.add)
                    last.then_inc(y_used, 1)
                    dve.wait_ge(y_used, y + 1)
                elif kind == "project":
                    b, j = s[1:]
                    y = y_no[s]
                    dve.wait_ge(y_full, y + 1)
                    if b and j == 0:
                        dve.wait_ge(beta_ready, b)
                    dve.tensor_tensor(qkvb[:, j, :], YB[y % 2][:, 0:PW], b_in[:, :], ALU.add)\
                       .then_inc(y_used, 1)
                    dve.wait_ge(y_used, y + 1)
                elif kind == "keys":
                    b = s[1]
                    k4 = qkvb[:, :, C:2 * C].rearrange("p j (h e) -> p j h e", h=H)
                    t4 = tmp[:, 0:BLK, :, :].rearrange("p a b e -> p (a b e)")
                    t3 = t4.rearrange("p (j c) -> p j c", j=BLK)
                    link(dve.tensor_tensor(t3, qkvb[:, :, C:2 * C], qkvb[:, :, C:2 * C], ALU.mult))
                    dve.tensor_reduce(flat(kn[:, 0, :, :]), t4.rearrange("p (a e) -> p a e", e=D), AX_X, ALU.add)\
                       .then_inc(length2_ready, 1)
                    dve.wait_ge(length_ready, b + 1)
                    link(dve.tensor_scalar(kn[:, 2, :, :], kn[:, 1, :, :], 1e-6, None, ALU.add))
                    link(dve.reciprocal(kn[:, 2, :, :], kn[:, 2, :, :]))

                    def spread(a):
                        return a.rearrange("p j (h o) -> p j h o", o=1).to_broadcast([P, BLK, H, D])

                    link(dve.tensor_tensor(k4, k4, spread(kn[:, 2, :, :]), ALU.mult))
                    dve.wait_ge(beta_ready, b + 1)
                    link(dve.tensor_scalar(kn[:, 0, :, :], beta[:, :, :], -1.0, None, ALU.mult))
                    link(dve.tensor_tensor(nkb[:, :, :].rearrange("p j (h e) -> p j h e", h=H), k4,
                                           spread(kn[:, 0, :, :]), ALU.mult))
                elif kind == "block":
                    b, j = s[1:]

                    def over_rows(a):
                        return a.rearrange("p (o c) -> p o c", o=1).to_broadcast([P, R, C])

                    k_j, q_j = over_rows(qkvb[:, j, C:2 * C]), over_rows(qkvb[:, j, 0:C])
                    v_j = qkvb[:, j, 2 * C:3 * C].rearrange("p (h d) -> p d h", h=H)
                    m3 = M[:, :, :, :].rearrange("p r h e -> p r (h e)")
                    t3 = tmp[:, :, :, :].rearrange("p r h e -> p r (h e)")
                    sums = tmp[:, :, :, :].rearrange("p r h e -> p (r h) e")
                    if j == 0:
                        if b:
                            dve.wait_ge(turn_full, 2 + turn_no["turn", "Q", b - 1, 1] + 1)
                        dve.tensor_scalar(dl[:, 0:D, :], v_j, -1.0, None, ALU.mult)
                        link(dve.tensor_copy(dl[:, D:R, :],
                                             qkvb[:, j, C:2 * C].rearrange("p (h d) -> p d h", h=H)))
                    else:
                        link(dve.tensor_tensor(t3, m3, k_j, ALU.mult))
                        link(dve.tensor_reduce(flat(dl[:, :, :]), sums, AX_X, ALU.add))
                        link(dve.tensor_tensor(dl[:, 0:D, :], dl[:, 0:D, :], v_j, ALU.subtract))
                    to = M if j == 0 else tmp
                    nkb_j = nkb[:, j, :].rearrange("p (o h e) -> p o h e", o=1, h=H).to_broadcast([P, R, H, D])
                    link(dve.tensor_tensor(to[:, :, :, :],
                                           dl[:, :, :].rearrange("p r (h o) -> p r h o", o=1)
                                           .to_broadcast([P, R, H, D]), nkb_j, ALU.mult))
                    if j == 0:
                        rows = M[:, D:R, :, :].rearrange("p r h e -> p (r h e)")
                        for e in range(D):
                            diag = rows[:, e * C + e:(e + 1) * C:D]
                            last = dve.tensor_scalar(diag, diag, 1.0, None, ALU.add)
                        link(last)
                    elif j < BLK - 1:
                        link(dve.tensor_tensor(m3, m3, t3, ALU.add))
                    else:
                        dve.tensor_tensor(m3, m3, t3, ALU.add).then_inc(blocks_done, 1)
                        dve.wait_ge(blocks_done, b + 1)
                    link(dve.tensor_tensor(t3, m3, q_j, ALU.mult))
                    link(dve.tensor_reduce(flat(res[:, b, j, :, :]), sums, AX_X, ALU.add))
                elif kind == "read":
                    b, j = s[1:]
                    if j == 0:
                        dve.wait_ge(turn_used, turned(("turn", "S", b, 1)))
                        if b:
                            dve.wait_ge(turn_full, 2 + turn_no["turn", "O", b - 1, 1] + 1)
                    t4 = tmp[:, 0:D, :, :]
                    back = res[:, b, j, D:R, :].rearrange("p e (o h) -> p o h e", o=1).to_broadcast([P, D, H, D])
                    o_j = O[:, j, :, :].rearrange("p h d -> p d h")
                    link(dve.tensor_tensor(t4, S[:, :, :, :], back, ALU.mult))
                    link(dve.tensor_reduce(o_j, t4, AX_X, ALU.add))
                    dve.tensor_tensor(o_j, o_j, res[:, b, j, 0:D, :], ALU.add).then_inc(o_ready, 1)
                    dve.wait_ge(o_ready, read_no[s] + 1)


_INS = ["L0_attn_a_residual", "L0_attn_a_w_fc", "L0_attn_a_w_proj", "L0_attn_a_ln_g", "L0_attn_a_ln_b",
        "L0_attn_b_Wq", "L0_attn_b_bq", "L0_attn_b_Wk", "L0_attn_b_bk", "L0_attn_b_Wv", "L0_attn_b_bv",
        "L0_attn_b_Wbeta", "L0_attn_b_bbeta", "L0_attn_b_Wo", "L0_attn_b_bo",
        "L0_ffn_W1", "L0_ffn_b1", "L0_ffn_W2", "L0_ffn_b2"]


def kernel(**inputs):
    import numpy as _np
    import concourse.bacc as _bacc
    from concourse import mybir as _mybir
    from concourse.bass_utils import run_bass_kernel_spmd as _run

    nc = _bacc.Bacc("TRN2", target_bir_lowering=False, num_devices=1)
    arrays, args = {}, []
    for name in _INS:
        a = _np.ascontiguousarray(inputs[name])
        arrays[f"in_{name}"] = a
        args.append(nc.dram_tensor(f"in_{name}", a.shape, _mybir.dt.from_np(a.dtype), kind="ExternalInput").ap())
    shape = inputs["L0_attn_a_residual"].shape
    args.append(nc.dram_tensor("out_0", shape, _mybir.dt.float32, kind="ExternalOutput").ap())
    layer_kernel(nc, *args)
    r = _run(nc, [arrays], core_ids=[0])
    return r.results[0]["out_0"]
```

```python
from contextlib import ExitStack

import concourse.bass as bass
from concourse import mybir

ALU = mybir.AluOpType
ACT = mybir.ActivationFunctionType
F32 = mybir.dt.float32
AX_X = mybir.AxisListType.X

P = 128
C = 128
NB = 2
BLK = 8
QT_ = 4
NT = 2
NQ = NT * BLK // QT_
GB = P // NB
NE = 8
FF = 512
FC = FF // P
AH = 4
AD = C // AH
NM = 4
H = 16
D = C // H
R = 2 * D
PW = 3 * C + H
SEG = 16
EPS = 1e-5
ROUND = 2.0 ** 23
ROUND_S = 1.5 * 2.0 ** 23


Y_STAGES = ("bias2", "bias2ed", "project", "out", "outed")


def spread(own, other):
    s, other, n_other, filling = [], list(other), len(other), False
    for n, stage in enumerate(own):
        s.append(stage)
        filling = stage[0] in ("down", "mix") or filling and stage[0] not in ("weigh", "mixed")
        while n_other - len(other) < n_other * (n + 1) // len(own):
            if filling and other[0][0] in Y_STAGES:
                break
            s.append(other.pop(0))
    return s + other


def attend_in(q):
    return [("stats", "Y", q), ("norm", "Y", q), ("stats", "Z", q), ("norm", "Z", q)]


def attend(q):
    s = [("turn", "x", "Z", q)]
    for h in range(AH):
        s.append(("score", q, h))
        if h:
            s.append(("mix", q, h - 1))
    return s + [("mix", q, AH - 1), ("mixed", q)]


def route(f):
    return [("stats", "F", f), ("norm", "F", f), ("route", f)]


def routed(f):
    return [("turn", "x", "F", f), ("turn", "w", f), ("bias2", f), ("bias2ed", f)]


def experts(f, more, before=None, last=False):
    s = []
    for e in range(NE + last):
        own = []
        if e < NE:
            own += [("up", f, e, c) for c in range(FC)]
        down = (f, e - 1) if e else before
        if down:
            own += [("down", *down, i) for i in range(QT_)] + [("weigh", *down)]
        s += spread(own, more.get(e, []))
    return s


def project(q):
    return [("turn", "x", "D", q)] + [("project", q, i) for i in range(QT_)] + [("lengths", q)]


def transfers(t):
    return ([("turn", "P", t, n) for n in range(2)] + [("turn", "Q", t, n) for n in range(2)]
            + [("unfold", t, n) for n in range(2)] + [("add", t)])


def chain(t):
    return [("state", t, g) for g in range(GB if t == 0 else GB - 1)]


def read_out(t):
    s = [("turn", "S", t, n) for n in range(2)]
    if t == 0:
        s.append(("carry", 0))
    s += [("read", t, j) for j in range(BLK)]
    for n in range(2):
        s += [("turn", "O", t, n), ("out", t, n), ("outed", t, n)]
    return s


def plan():
    def block(t, *js):
        return [("block", t, j) for j in js]

    def norm_d(q):
        return [("stats", "D", q), ("norm", "D", q)]

    s = [("stats", "Y", 0), ("norm", "Y", 0), ("stats", "Z", 0), ("stats", "Y", 1), ("norm", "Z", 0),
         ("norm", "Y", 1), ("stats", "Z", 1)]
    s += attend(0)[:3] + [("norm", "Z", 1)] + attend(0)[3:]
    a1 = attend(1)
    s += a1[:2] + route(0)[:1] + a1[2:4] + route(0)[1:] + a1[4:] + route(1)[:1] + routed(0)
    s += experts(0, {0: route(1)[1:], 3: routed(1), 4: attend_in(2), 6: attend_in(3)})
    s += experts(1, {1: norm_d(0) + project(0) + [("turn", "x", "Z", 2)], 2: [("turn", "x", "Z", 3)], 3: [("keys", 0)] + block(0, 0), 5: block(0, 1),
                     7: block(0, 2)}, before=(0, NE - 1), last=True)
    s += norm_d(1) + attend(2)[1:3] + project(1) + attend(2)[3:]
    s += route(2)[:1] + block(0, 3) + [("keys", 1)] + route(2)[1:]
    s += spread(attend(3)[1:], block(0, 4, 5)) + routed(2) + route(3)
    s += experts(2, {0: block(0, 6), 2: block(0, 7), 3: routed(3), 4: transfers(0)})
    c0 = chain(0)
    s += experts(3, {0: c0[:8], 1: norm_d(2) + c0[8:16] + project(2), 2: c0[16:24] + [("keys", 2)], 3: c0[24:34] + block(1, 0), 4: c0[34:44], 5: c0[44:54] + block(1, 1), 6: c0[54:]},
                 before=(2, NE - 1), last=True)
    s += read_out(0)
    s += route(4) + norm_d(3) + routed(4) + project(3)
    s += experts(4, {0: block(1, 2) + [("keys", 3)], 2: block(1, 3), 4: block(1, 4), 5: route(5), 6: routed(5), 7: block(1, 5)})
    c1 = chain(1)
    s += experts(5, {0: block(1, 6), 2: block(1, 7), 3: transfers(1)} | {e: c1[16 * (e - 4):16 * (e - 3)] for e in range(4, 8)},
                 before=(4, NE - 1), last=True)
    s += read_out(1) + route(6) + routed(6)
    s += experts(6, {1: route(7), 4: routed(7)}) + experts(7, {}, before=(6, NE - 1), last=True)
    return s


def layer_kernel(nc, residual, w_fc, w_proj, ln_g, ln_b, Wq, bq, Wk, bk, Wv, bv, Wbeta, bbeta, Wo, bo,
                 W1, b1, W2, b2, out):
    stages = plan()

    def order(*kinds):
        return {s: n for n, s in enumerate(x for x in stages if x[0] in kinds)}

    norm_no = order("norm")
    turn_no = order("turn")
    turns = 2 + len(turn_no)
    score_no = order("score")
    up_no = order("up")
    y_no = {}
    for s in stages:
        if s[0] == "mix" and s[2] == 0:
            y_no["mix", s[1]] = len(y_no)
        elif s[0] in ("bias2", "project", "out"):
            y_no[s] = len(y_no)
        elif s[0] == "down" and s[3] == 0:
            y_no["down", s[1], s[2]] = len(y_no)
    z_no, z = {}, 0
    for s in stages:
        if s[0] == "score":
            z_no[s] = z
            z += NM
        elif s[0] == "up":
            z_no[s] = z
            z += 1
    block_no, state_no, unfold_no, read_no = order("block"), order("state"), order("unfold"), order("read")
    out_no = order("out")

    with ExitStack() as ctx:
        def sb(name, shape):
            return ctx.enter_context(nc.sbuf_tensor(name, [P, *shape], F32))

        def bank(name):
            return ctx.enter_context(nc.psum_tensor(name, [P, 512], F32))

        def sem(name):
            return ctx.enter_context(nc.semaphore(name))

        X = sb("X", [NB * BLK, C])
        w1 = sb("w1", [NE, FF])
        w2 = sb("w2", [NE, FC, C])
        b1_rows = sb("b1_rows", [P])
        b1_cols = sb("b1_cols", [NE * FC])
        b2_rows = sb("b2_rows", [C])
        wfc = sb("wfc", [C])
        wproj = sb("wproj", [C])
        wfc4 = sb("wfc4", [NM, AH, AD])
        table_k = sb("table_k", [NM, AH, P])
        table_v = sb("table_v", [NM, AD])
        gain = sb("gain", [1])
        shift = sb("shift", [1])
        w_in = sb("w_in", [PW])
        b_in = sb("b_in", [PW])
        w_out = sb("w_out", [C])
        b_out = sb("b_out", [C])
        ones = sb("ones", [P])
        ident = sb("ident", [P])
        numbers = sb("numbers", [NE])
        halves = sb("halves", [2 * P])
        stat = sb("stat", [2, QT_, 6])
        mv = sb("mv", [2, QT_, 2])
        var_eps = sb("var_eps", [2, QT_])
        rstd = sb("rstd", [2, QT_])
        YN = sb("YN", [4, QT_, C])
        zT = sb("zT", [2, QT_ * P])
        dT = sb("dT", [2, QT_ * P])
        xT = sb("xT", [4, QT_ * P])
        rt = sb("rt", [8, QT_])
        hit = sb("hit", [QT_, NE])
        wt = sb("wt", [4, QT_, NE])
        wT = sb("wT", [2, QT_ * P])
        hid = sb("hid", [2, 4, 512])
        qkvb = sb("qkvb", [BLK, PW])
        nkb = sb("nkb", [BLK, C])
        beta = sb("beta", [QT_, H])
        kn = sb("kn", [3, QT_, H])
        M = sb("M", [R, H, D])
        tmp = sb("tmp", [R, H, D])
        dl = sb("dl", [R, H])
        res = sb("res", [NB, BLK, R, H])
        pT = sb("pT", [D, P])
        qT = sb("qT", [D, P])
        first = sb("first", [NB, D])
        unfolded = sb("unfolded", [2, H, D, NB, SEG])
        ST = sb("ST", [D, P])
        S = sb("S", [D, H, D])
        O = sb("O", [BLK, H, D])
        oT = pT

        TB = [bank(f"TB{i}") for i in range(2)]
        ZB = [bank(f"ZB{i}") for i in range(2)]
        YB = [bank(f"YB{i}") for i in range(2)]
        CB = ctx.enter_context(nc.psum_tensor("CB", [P, NB, GB, D], F32))

        x_in = [sem(f"x_in{q}") for q in range(NQ)]
        consts_in = sem("consts_in")
        w_in_in = sem("w_in_in")
        ff_in = sem("ff_in")
        pool_consts = sem("pool_consts")
        ident_ready = sem("ident_ready")
        var_ready = sem("var_ready")
        eps_added = sem("eps_added")
        rstd_ready = sem("rstd_ready")
        norm_ready = sem("norm_ready")
        wfc4_ready = sem("wfc4_ready")
        turn_full = sem("turn_full")
        turn_used = sem("turn_used")
        z_full = sem("z_full")
        z_used = sem("z_used")
        squared = sem("squared")
        y_full = sem("y_full")
        y_used = sem("y_used")
        route_ready = sem("route_ready")
        beta_ready = sem("beta_ready")
        keys_ready = sem("keys_ready")
        length2_ready = sem("length2_ready")
        length_ready = sem("length_ready")
        blocks_done = sem("blocks_done")
        unfold_zeroed = sem("unfold_zeroed")
        unfold_in = [sem(f"unfold_in{i}") for i in range(2)]
        state_full = sem("state_full")
        state_ready = sem("state_ready")
        o_ready = sem("o_ready")
        stored = sem("stored")
        dve_done = sem("dve_done")

        N_SMALL = 7

        def quad(t, q):
            return t[:, q * QT_:(q + 1) * QT_, :]

        def flat(ap):
            return ap.rearrange("p a b -> p (a b)")

        def x_dram(a, q, b):
            t, half = divmod(q, 2)
            return a[b].rearrange("(t g j) c -> t g j c", t=NT, j=BLK)[t, :, half * QT_:(half + 1) * QT_, :]

        def x_rows(q, b):
            return X[b * GB:(b + 1) * GB, q * QT_:(q + 1) * QT_, :]

        def turned(s):
            return 2 + turn_no[s] + 1

        block = ctx.enter_context(nc.Block())

        @block.sync
        def _(sp):
            for b in range(NB):
                sp.dma_start(x_rows(0, b), x_dram(residual, 0, b)).then_inc(x_in[0], 16)
            sp.dma_start(wfc[:, :], w_fc).then_inc(consts_in, 16)
            sp.dma_start(wproj[:, :], w_proj).then_inc(consts_in, 16)
            sp.dma_start(gain[:, :], ln_g.rearrange("(c o) -> c o", o=1)).then_inc(consts_in, 16)
            sp.dma_start(shift[:, :], ln_b.rearrange("(c o) -> c o", o=1)).then_inc(consts_in, 16)
            sp.dma_start(b1_rows[0:NE * FC, :], b1.rearrange("e (c p) -> (e c) p", p=P)).then_inc(consts_in, 16)
            sp.dma_start(b2_rows[0:NE, :], b2).then_inc(consts_in, 16)
            sp.dma_start(b_out[0:1, :], bo.rearrange("(o c) -> o c", o=1)).then_inc(consts_in, 16)
            for q in range(1, NQ):
                for b in range(NB):
                    sp.dma_start(x_rows(q, b), x_dram(residual, q, b)).then_inc(x_in[q], 16)
            for e in range(NE):
                sp.dma_start(w1[:, e, :], W1[e]).then_inc(ff_in, 16)
                sp.dma_start(w2[:, e, :, :], W2[e].rearrange("(c p) d -> p c d", p=P)).then_inc(ff_in, 16)
            at = 0
            for w, bias in ((Wq, bq), (Wk, bk), (Wv, bv), (Wbeta, bbeta)):
                n = w.shape[1]
                sp.dma_start(w_in[:, at:at + n], w).then_inc(w_in_in, 16)
                sp.dma_start(b_in[:, at:at + n],
                             bias.rearrange("(o c) -> o c", o=1).broadcast_to([P, n])).then_inc(w_in_in, 16)
                at += n
            sp.dma_start(w_out[:, :], Wo).then_inc(w_in_in, 16)

            def unfold(t, seg):
                n = t * (GB // SEG) + seg
                if n >= 2:
                    was, part = divmod(n - 2, GB // SEG)
                    last = min((part + 1) * SEG, GB if was == 0 else GB - 1) - 1
                    sp.wait_ge(state_full, state_no["state", was, last] + 1)
                sp.wait_ge(turn_used, turned(("turn", "P", t, 1)))
                for h in range(H):
                    sp.dma_start(unfolded[h * D:(h + 1) * D, n % 2, h, :, :, :],
                                 pT[h:P:H, :, :].rearrange("x e (b g) -> x e b g", b=NB)
                                 [:, :, :, seg * SEG:(seg + 1) * SEG]).then_inc(unfold_in[n % 2], 16)

            sp.wait_ge(unfold_zeroed, 1)
            for s in stages:
                if s[0] == "unfold":
                    unfold(s[1], s[2])
                elif s[0] == "state" and s[2] in (SEG, 2 * SEG):
                    unfold(s[1], s[2] // SEG + 1)
            for q in range(NQ):
                sp.wait_ge(y_used, y_no["down", NQ + q, NE - 1] + 1)
                for b in range(NB):
                    sp.dma_start(x_dram(out, q, b), x_rows(q, b)).then_inc(stored, 16)
            sp.wait_ge(stored, 16 * NQ * NB)

        @block.gpsimd
        def _(pool):
            pool.memset(ident[:, :], 1.0).then_inc(pool_consts, 1)
            pool.wait_ge(pool_consts, 1)
            pool.affine_select(out=ident[:, :], in_=ident[:, :], compare_op=ALU.is_equal, fill=0.0, base=0,
                               pattern=[[-1, P]], channel_multiplier=1).then_inc(ident_ready, 1)
            pool.memset(halves[:, 0:P], -0.5)
            pool.memset(halves[:, P:2 * P], 0.5).then_inc(pool_consts, 1)
            pool.wait_ge(pool_consts, 2)
            pool.memset(table_k[:, :, :, :], 0.0)
            pool.memset(ones[:, :], 1.0)
            pool.iota(numbers[:, :], pattern=[[1, NE]], base=0, channel_multiplier=0,
                      allow_small_or_imprecise_dtypes=True)
            pool.memset(ST[:, :, 0:P:GB], 0.0).then_inc(pool_consts, 1)
            unfold_set = False
            for s in stages:
                if s[0] == "stats":
                    n = norm_no["norm", s[1], s[2]]
                    pool.wait_ge(var_ready, n + 1)
                    pool.tensor_scalar(var_eps[:, n % 2, :], mv[:, n % 2, :, 1], EPS, 1.0, ALU.add,
                                       ALU.mult).then_inc(eps_added, 1)
                    pool.wait_ge(eps_added, n + 1)
                    pool.tensor_tensor(rstd[:, n % 2, :], var_eps[:, n % 2, :], halves[:, 0:QT_],
                                       ALU.pow).then_inc(rstd_ready, 1)
                elif s[0] == "lengths":
                    pool.wait_ge(length2_ready, s[1] + 1)
                    pool.tensor_tensor(flat(kn[:, 1, :, :]), flat(kn[:, 0, :, :]), halves[:, P:P + QT_ * H],
                                       ALU.pow).then_inc(length_ready, 1)
                if not unfold_set and s[0] == "up":
                    unfold_set = True
                    pool.memset(unfolded[:, :, :, :, :, :], 0.0).then_inc(unfold_zeroed, 1)

        @block.tensor
        def _(pe):
            fills = [0]

            def turn(parts, n):
                bank_ = TB[n % 2]
                if n >= 2:
                    pe.wait_ge(turn_used, n - 1)
                for at, ap, rows, cols in parts:
                    last = pe.transpose(bank_[0:rows, at:at + cols], ap, ident[0:cols, 0:cols])
                last.then_inc(turn_full, 1)

            def y_bank(key):
                n = y_no[key]
                if n >= 2:
                    pe.wait_ge(y_used, n - 1)
                return YB[n % 2]

            pe.wait_ge(ident_ready, 1)
            pe.wait_ge(consts_in, 16 * N_SMALL)
            pe.wait_ge(wfc4_ready, 1)
            turn([(m * P, flat(wfc4[:, m, :, :]), P, P) for m in range(NM)], 0)
            turn([(0, wproj[:, :], P, P), (P, b1_rows[0:NE * FC, :], P, NE * FC)], 1)
            pe.wait_ge(pool_consts, 3)
            unfolds = 0
            for s in stages:
                kind = s[0]
                if kind == "turn":
                    n = 2 + turn_no[s]
                    what = s[1]
                    if what == "x":
                        k = norm_no["norm", s[2], s[3]]
                        pe.wait_ge(norm_ready, k + 1)
                        turn([(i * P, YN[:, k % 4, i, :], P, P) for i in range(QT_)], n)
                    elif what == "w":
                        pe.wait_ge(route_ready, s[2] + 1)
                        turn([(i * P, wt[:, s[2] % 4, i, :], NE, P) for i in range(QT_)], n)
                    elif what == "P":
                        pe.wait_ge(blocks_done, s[2] + 1)
                        turn([(i * P, flat(M[:, D:R, :, 4 * s[3] + i]), P, P) for i in range(4)], n)
                    elif what == "Q":
                        pe.wait_ge(blocks_done, s[2] + 1)
                        turn([(i * P, flat(M[:, 4 * s[3] + i, :, :]), P, P) for i in range(4)], n)
                    elif what == "S":
                        pe.wait_ge(state_ready, GB if s[2] == 0 else 2 * GB)
                        turn([(i * P, ST[:, 4 * s[3] + i, :], P, P) for i in range(4)], n)
                    elif what == "O":
                        pe.wait_ge(o_ready, read_no["read", s[2], 4 * s[3] + 3] + 1)
                        turn([(i * P, O[:, 4 * s[3] + i, :, :].rearrange("p h d -> p (h d)"), P, P)
                              for i in range(4)], n)
                elif kind == "score":
                    q, h = s[1:]
                    pe.wait_ge(turn_used, turned(("turn", "x", "Z", q)))
                    for m in range(NM):
                        z = z_no[s] + m
                        if z >= 2:
                            pe.wait_ge(z_used, z - 1)
                        pe.matmul(ZB[z % 2][:, :], table_k[:, m, h, :], zT[:, q % 2, :], start=True,
                                  stop=True).then_inc(z_full, 1)
                elif kind == "mix":
                    q, h = s[1:]
                    k = score_no["score", q, h]
                    if h == 0:
                        y_bank(("mix", q))
                    yb = YB[y_no["mix", q] % 2]
                    pe.wait_ge(squared, NM * (k + 1))
                    for i in range(QT_):
                        for m in range(NM):
                            last = pe.matmul(yb[:, i * C + h * AD:i * C + (h + 1) * AD],
                                             hid[:, k % 2, m, i * P:(i + 1) * P], table_v[:, m, :],
                                             start=(m == 0), stop=(m == NM - 1))
                    if h == AH - 1:
                        last.then_inc(y_full, 1)
                elif kind == "bias2":
                    f = s[1]
                    pe.wait_ge(turn_used, turned(("turn", "w", f)))
                    yb = y_bank(s)
                    for i in range(QT_):
                        last = pe.matmul(yb[:, i * C:(i + 1) * C], wT[0:NE, f % 2, i * P:(i + 1) * P],
                                         b2_rows[0:NE, :], start=True, stop=True)
                    last.then_inc(y_full, 1)
                elif kind == "up":
                    f, e, c = s[1:]
                    if e == 0 and c == 0:
                        pe.wait_ge(ff_in, 16 * 2 * NE)
                        pe.wait_ge(turn_used, turned(("turn", "x", "F", f)))
                    z = z_no[s]
                    if z >= 2:
                        pe.wait_ge(z_used, z - 1)
                    pe.matmul(ZB[z % 2][:, :], w1[:, e, c * P:(c + 1) * P], xT[:, f % 4, :], start=True,
                              stop=True).then_inc(z_full, 1)
                elif kind == "down":
                    f, e, i = s[1:]
                    u = f * NE + e
                    if i == 0:
                        y_bank(("down", f, e))
                        pe.wait_ge(z_used, z_no["up", f, e, FC - 1] + 1)
                    yb = YB[y_no["down", f, e] % 2]
                    for c in range(FC):
                        last = pe.matmul(yb[:, i * C:(i + 1) * C], hid[:, u % 2, c, i * P:(i + 1) * P],
                                         w2[:, e, c, :], start=(c == 0), stop=(c == FC - 1))
                    if i == QT_ - 1:
                        last.then_inc(y_full, 1)
                elif kind == "project":
                    q, i = s[1:]
                    if i == 0:
                        pe.wait_ge(w_in_in, 16 * 9)
                        pe.wait_ge(turn_used, turned(("turn", "x", "D", q)))
                    pe.matmul(y_bank(s)[:, 0:PW], dT[:, q % 2, i * P:(i + 1) * P], w_in[:, :], start=True,
                              stop=True).then_inc(y_full, 1)
                elif kind == "add":
                    t = s[1]
                    pe.wait_ge(turn_used, turned(("turn", "Q", t, 1)))
                    if t:
                        pe.wait_ge(state_ready, GB)
                    for b in range(NB):
                        pe.matmul(CB[:, b, :, :], ident[:, :],
                                  qT[:, :, b * GB:(b + 1) * GB].rearrange("p d g -> p g d"),
                                  start=True, stop=True)
                elif kind == "state":
                    t, g = s[1:]
                    n = t * (GB // SEG) + g // SEG
                    if g % SEG == 0:
                        pe.wait_ge(unfold_in[n % 2], 16 * H * (n // 2 + 1))
                    if t or g:
                        pe.wait_ge(state_ready, t * (GB + 1) + g)
                    for b in range(NB):
                        last = pe.matmul(CB[:, b, g, :],
                                         unfolded[:, n % 2, :, :, b, g % SEG].rearrange("p h e -> p (h e)"),
                                         ST[:, :, b * GB + g], start=False, stop=True, skip_group_check=True)
                    last.then_inc(state_full, 1)
                elif kind == "out":
                    b, n = s[1:]
                    pe.wait_ge(turn_used, turned(("turn", "O", b, n)))
                    yb = y_bank(s)
                    for i in range(QT_):
                        pe.matmul(yb[:, i * C:(i + 1) * C], ones[0:1, :], b_out[0:1, :], start=True, stop=False)
                        last = pe.matmul(yb[:, i * C:(i + 1) * C], oT[:, n * QT_ + i, :], w_out[:, :],
                                         start=False, stop=True)
                    last.then_inc(y_full, 1)

        @block.scalar
        def _(act):
            act.wait_ge(pool_consts, 3)
            act.wait_ge(turn_full, 1)
            for h in range(AH):
                rows = slice(h * AD, (h + 1) * AD)
                last = act.activation(table_k[rows, :, h, :], TB[0][rows, :].rearrange("p (m c) -> p m c", m=NM),
                                      ACT.Copy)
            last.then_inc(turn_used, 1)
            act.wait_ge(turn_full, 2)
            act.activation(table_v[:, :, :], TB[1][:, 0:C].rearrange("p (m d) -> p m d", m=NM), ACT.Copy)
            act.activation(b1_cols[:, :], TB[1][:, P:P + NE * FC], ACT.Copy).then_inc(turn_used, 1)
            for s in stages:
                kind = s[0]
                if kind == "turn":
                    n = 2 + turn_no[s]
                    act.wait_ge(turn_full, n + 1)
                    tb = TB[n % 2]
                    four = tb[:, :].rearrange("p (i t) -> p i t", i=4)
                    what = s[1]
                    if what == "x" and s[2] == "Z":
                        act.wait_ge(consts_in, 16 * N_SMALL)
                        ins = act.activation(zT[:, s[3] % 2, :], tb[:, :], ACT.Identity, bias=shift[:, 0:1],
                                             scale=gain[:, 0:1])
                    elif what == "x" and s[2] == "F":
                        ins = act.activation(xT[:, s[3] % 4, :], tb[:, :], ACT.Copy)
                    elif what == "x":
                        ins = act.activation(dT[:, s[3] % 2, :], tb[:, :], ACT.Copy)
                    elif what == "w":
                        ins = act.activation(wT[0:NE, s[2] % 2, :], tb[0:NE, :], ACT.Copy)
                    elif what == "P":
                        ins = act.activation(pT[:, 4 * s[3]:4 * s[3] + 4, :], four, ACT.Copy)
                    elif what == "Q":
                        ins = act.activation(qT[:, 4 * s[3]:4 * s[3] + 4, :], four, ACT.Copy)
                    elif what == "S":
                        ins = act.activation(S[:, 4 * s[3]:4 * s[3] + 4, :, :],
                                             tb[:, :].rearrange("p (d h e) -> p d h e", d=4, h=H), ACT.Copy)
                    elif what == "O":
                        ins = act.activation(oT[:, 4 * s[3]:4 * s[3] + 4, :], four, ACT.Copy)
                    ins.then_inc(turn_used, 1)
                elif kind == "score":
                    k = score_no[s]
                    for m in range(NM + 1):
                        if m < NM:
                            z = z_no[s] + m
                            act.wait_ge(z_full, z + 1)
                            act.activation(hid[:, k % 2, m, :], ZB[z % 2][:, :], ACT.Relu).then_inc(z_used, 1)
                        if m:
                            act.wait_ge(z_used, z_no[s] + m)
                            act.activation(hid[:, k % 2, m - 1, :], hid[:, k % 2, m - 1, :], ACT.Square)\
                               .then_inc(squared, 1)
                elif kind == "up":
                    f, e, c = s[1:]
                    u = f * NE + e
                    z = z_no[s]
                    act.wait_ge(z_full, z + 1)
                    n = e * FC + c
                    act.activation(hid[:, u % 2, c, :], ZB[z % 2][:, :], ACT.Relu,
                                   bias=b1_cols[:, n:n + 1]).then_inc(z_used, 1)
                elif kind == "lengths":
                    q = s[1]
                    act.wait_ge(y_used, y_no["project", q, QT_ - 1] + 1)
                    if q:
                        act.wait_ge(keys_ready, q)
                    act.activation(beta[:, :, :], qkvb[:, (q % 2) * QT_:(q % 2 + 1) * QT_, 3 * C:PW], ACT.Sigmoid).then_inc(beta_ready, 1)
                elif kind == "state":
                    t, g = s[1:]
                    act.wait_ge(state_full, state_no[s] + 1)
                    to = ST[:, :, g + 1:P:GB].rearrange("p d b -> p b d") if g < GB - 1 else first[:, :, :]
                    act.activation(to, CB[:, :, g, :], ACT.Copy).then_inc(state_ready, 1)
                elif kind == "carry":
                    act.wait_ge(turn_full, 2 + turn_no["turn", "S", 0, 1] + 1)
                    act.wait_ge(state_ready, GB)
                    act.activation(ST[:, :, 0:P:GB].rearrange("p d b -> p b d"), first[:, :, :], ACT.Copy)\
                       .then_inc(state_ready, 1)

        @block.vector
        def _(dve):
            links = [0]

            def link(ins):
                links[0] += 1
                ins.then_inc(dve_done, 1)
                dve.wait_ge(dve_done, links[0])

            dve.wait_ge(consts_in, 16 * N_SMALL)
            for m in range(NM):
                last = dve.tensor_copy(wfc4[:, m, :, :], wfc[:, m * AD:(m + 1) * AD]
                                       .rearrange("p (o d) -> p o d", o=1).to_broadcast([P, AH, AD]))
            last.then_inc(wfc4_ready, 1)
            dve.wait_ge(pool_consts, 3)
            for s in stages:
                kind = s[0]
                if kind == "stats":
                    what, q = s[1:]
                    n = norm_no["norm", what, q]
                    if what == "Y":
                        dve.wait_ge(x_in[q], 16 * NB)
                    src = YN[:, norm_no["norm", "Y", q] % 4, :, :] if what == "Z" else quad(X, q % NQ)
                    for i in range(QT_):
                        last = dve.bn_stats(stat[:, n % 2, i, :], src[:, i, :])
                    link(last)
                    for i in range(QT_):
                        last = dve.bn_aggr(mv[:, n % 2, i, :], stat[:, n % 2, i, :])
                    last.then_inc(var_ready, 1)
                elif kind == "norm":
                    what, q = s[1:]
                    n = norm_no[s]
                    src = YN[:, norm_no["norm", "Y", q] % 4, :, :] if what == "Z" else quad(X, q % NQ)
                    dve.wait_ge(rstd_ready, n + 1)
                    old = [t for t in turn_no if t[1] == "x" and norm_no["norm", t[2], t[3]] == n - 4]
                    if old:
                        dve.wait_ge(turn_full, 2 + turn_no[old[0]] + 1)
                    for i in range(QT_):
                        last = dve.tensor_scalar(YN[:, n % 4, i, :], src[:, i, :], mv[:, n % 2, i, 0:1],
                                                 rstd[:, n % 2, i:i + 1], ALU.subtract, ALU.mult)
                    last.then_inc(norm_ready, 1)
                    dve.wait_ge(norm_ready, n + 1)
                    if what == "Y":
                        link(dve.tensor_tensor(flat(quad(X, q)), flat(quad(X, q)), flat(YN[:, n % 4, :, :]),
                                               ALU.add))
                elif kind in ("mixed", "bias2ed", "outed"):
                    if kind == "mixed":
                        y, q = y_no["mix", s[1]], s[1]
                    elif kind == "bias2ed":
                        y, q = y_no["bias2", s[1]], s[1] % NQ
                    else:
                        y, q = y_no["out", s[1], s[2]], 2 * s[1] + s[2]
                    dve.wait_ge(y_full, y + 1)
                    link_to = dve.tensor_tensor(flat(quad(X, q)), flat(quad(X, q)), YB[y % 2][:, :], ALU.add)
                    link_to.then_inc(y_used, 1)
                    dve.wait_ge(y_used, y + 1)
                elif kind == "route":
                    f = s[1]
                    y = YN[:, norm_no["norm", "F", f] % 4, :, :]
                    sm, ab, rd, up_, fl, ng, t8, hh = (rt[:, i, :] for i in range(8))
                    link(dve.tensor_tensor(sm, y[:, :, 0], y[:, :, 1], ALU.add))
                    link(dve.scalar_tensor_tensor(out=ab, in0=sm, scalar=-1.0, in1=sm, op0=ALU.mult, op1=ALU.max))
                    link(dve.tensor_scalar(rd, ab, ROUND, None, ALU.add))
                    link(dve.tensor_scalar(rd, rd, ROUND, None, ALU.subtract))
                    link(dve.tensor_tensor(up_, rd, ab, ALU.is_gt))
                    link(dve.tensor_tensor(fl, rd, up_, ALU.subtract))
                    link(dve.tensor_scalar(ng, sm, 0.0, -2.0, ALU.is_lt, ALU.mult))
                    link(dve.scalar_tensor_tensor(out=hh, in0=ng, scalar=1.0, in1=fl, op0=ALU.add, op1=ALU.mult))
                    link(dve.tensor_scalar(t8, hh, 1.0 / NE, None, ALU.mult))
                    link(dve.tensor_scalar(rd, t8, ROUND_S, None, ALU.add))
                    link(dve.tensor_scalar(rd, rd, ROUND_S, None, ALU.subtract))
                    link(dve.tensor_tensor(up_, rd, t8, ALU.is_gt))
                    link(dve.tensor_tensor(fl, rd, up_, ALU.subtract))
                    link(dve.scalar_tensor_tensor(out=hh, in0=fl, scalar=-float(NE), in1=hh, op0=ALU.mult,
                                                  op1=ALU.add))
                    link(dve.tensor_tensor(hit[:, :, :],
                                           hh.rearrange("p (i o) -> p i o", o=1).to_broadcast([P, QT_, NE]),
                                           numbers[:, :].rearrange("p (o e) -> p o e", o=1)
                                           .to_broadcast([P, QT_, NE]), ALU.is_equal))
                    w = wt[:, f % 4, :, :]
                    link(dve.tensor_scalar(hit[:, :, :], hit[:, :, :], 0.5, None, ALU.mult))
                    if f >= 4:
                        dve.wait_ge(turn_full, 2 + turn_no["turn", "w", f - 4] + 1)
                    dve.tensor_tensor(w[:, :, 1:NE], hit[:, :, 1:NE], hit[:, :, 0:NE - 1], ALU.add)
                    dve.tensor_tensor(w[:, :, 0:1], hit[:, :, 0:1], hit[:, :, NE - 1:NE], ALU.add)\
                       .then_inc(route_ready, 1)
                    dve.wait_ge(route_ready, f + 1)
                elif kind == "weigh":
                    f, e = s[1:]
                    y = y_no["down", f, e]
                    dve.wait_ge(y_full, y + 1)
                    for i in range(QT_):
                        xq = X[:, (f % NQ) * QT_ + i, :]
                        last = dve.scalar_tensor_tensor(out=xq, in0=YB[y % 2][:, i * C:(i + 1) * C],
                                                        scalar=wt[:, f % 4, i, e:e + 1], in1=xq, op0=ALU.mult,
                                                        op1=ALU.add)
                    last.then_inc(y_used, 1)
                    dve.wait_ge(y_used, y + 1)
                elif kind == "project":
                    q, i = s[1:]
                    y = y_no[s]
                    dve.wait_ge(y_full, y + 1)
                    dve.tensor_tensor(qkvb[:, (q % 2) * QT_ + i, :], YB[y % 2][:, 0:PW], b_in[:, :], ALU.add)\
                       .then_inc(y_used, 1)
                    dve.wait_ge(y_used, y + 1)
                elif kind == "lengths":
                    q = s[1]
                    js = slice((q % 2) * QT_, (q % 2 + 1) * QT_)
                    k3 = qkvb[:, js, C:2 * C]
                    t4 = tmp[:, 0:QT_, :, :].rearrange("p a b e -> p (a b e)")
                    link(dve.tensor_tensor(t4.rearrange("p (j c) -> p j c", j=QT_), k3, k3, ALU.mult))
                    dve.tensor_reduce(flat(kn[:, 0, :, :]), t4.rearrange("p (a e) -> p a e", e=D), AX_X, ALU.add)\
                       .then_inc(length2_ready, 1)
                    dve.wait_ge(length2_ready, q + 1)
                elif kind == "keys":
                    q = s[1]
                    js = slice((q % 2) * QT_, (q % 2 + 1) * QT_)
                    k4 = qkvb[:, js, C:2 * C].rearrange("p j (h e) -> p j h e", h=H)
                    dve.wait_ge(length_ready, q + 1)
                    link(dve.tensor_scalar(kn[:, 2, :, :], kn[:, 1, :, :], 1e-6, None, ALU.add))
                    link(dve.reciprocal(kn[:, 2, :, :], kn[:, 2, :, :]))

                    def over_row(a):
                        return a.rearrange("p j (h o) -> p j h o", o=1).to_broadcast([P, QT_, H, D])

                    link(dve.tensor_tensor(k4, k4, over_row(kn[:, 2, :, :]), ALU.mult))
                    dve.wait_ge(beta_ready, q + 1)
                    link(dve.tensor_scalar(kn[:, 0, :, :], beta[:, :, :], -1.0, None, ALU.mult))
                    dve.tensor_tensor(nkb[:, js, :].rearrange("p j (h e) -> p j h e", h=H), k4,
                                      over_row(kn[:, 0, :, :]), ALU.mult).then_inc(keys_ready, 1)
                    dve.wait_ge(keys_ready, q + 1)
                elif kind == "block":
                    b, j = s[1:]

                    def over_rows(a):
                        return a.rearrange("p (o c) -> p o c", o=1).to_broadcast([P, R, C])

                    k_j, q_j = over_rows(qkvb[:, j, C:2 * C]), over_rows(qkvb[:, j, 0:C])
                    v_j = qkvb[:, j, 2 * C:3 * C].rearrange("p (h d) -> p d h", h=H)
                    m3 = M[:, :, :, :].rearrange("p r h e -> p r (h e)")
                    t3 = tmp[:, :, :, :].rearrange("p r h e -> p r (h e)")
                    sums = tmp[:, :, :, :].rearrange("p r h e -> p (r h) e")
                    if j == 0:
                        if b:
                            dve.wait_ge(turn_full, 2 + turn_no["turn", "Q", b - 1, 1] + 1)
                        dve.tensor_scalar(dl[:, 0:D, :], v_j, -1.0, None, ALU.mult)
                        link(dve.tensor_copy(dl[:, D:R, :],
                                             qkvb[:, j, C:2 * C].rearrange("p (h d) -> p d h", h=H)))
                    else:
                        link(dve.tensor_tensor(t3, m3, k_j, ALU.mult))
                        link(dve.tensor_reduce(flat(dl[:, :, :]), sums, AX_X, ALU.add))
                        link(dve.tensor_tensor(dl[:, 0:D, :], dl[:, 0:D, :], v_j, ALU.subtract))
                    to = M if j == 0 else tmp
                    nkb_j = nkb[:, j, :].rearrange("p (o h e) -> p o h e", o=1, h=H).to_broadcast([P, R, H, D])
                    link(dve.tensor_tensor(to[:, :, :, :],
                                           dl[:, :, :].rearrange("p r (h o) -> p r h o", o=1)
                                           .to_broadcast([P, R, H, D]), nkb_j, ALU.mult))
                    if j == 0:
                        rows = M[:, D:R, :, :].rearrange("p r h e -> p (r h e)")
                        for e in range(D):
                            diag = rows[:, e * C + e:(e + 1) * C:D]
                            last = dve.tensor_scalar(diag, diag, 1.0, None, ALU.add)
                        link(last)
                    elif j < BLK - 1:
                        link(dve.tensor_tensor(m3, m3, t3, ALU.add))
                    else:
                        dve.tensor_tensor(m3, m3, t3, ALU.add).then_inc(blocks_done, 1)
                        dve.wait_ge(blocks_done, b + 1)
                    link(dve.tensor_tensor(t3, m3, q_j, ALU.mult))
                    link(dve.tensor_reduce(flat(res[:, b, j, :, :]), sums, AX_X, ALU.add))
                elif kind == "read":
                    b, j = s[1:]
                    if j == 0:
                        dve.wait_ge(turn_used, turned(("turn", "S", b, 1)))
                        if b:
                            dve.wait_ge(turn_full, 2 + turn_no["turn", "O", b - 1, 1] + 1)
                    t4 = tmp[:, 0:D, :, :]
                    back = res[:, b, j, D:R, :].rearrange("p e (o h) -> p o h e", o=1).to_broadcast([P, D, H, D])
                    o_j = O[:, j, :, :].rearrange("p h d -> p d h")
                    link(dve.tensor_tensor(t4, S[:, :, :, :], back, ALU.mult))
                    link(dve.tensor_reduce(o_j, t4, AX_X, ALU.add))
                    dve.tensor_tensor(o_j, o_j, res[:, b, j, 0:D, :], ALU.add).then_inc(o_ready, 1)
                    dve.wait_ge(o_ready, read_no[s] + 1)


_INS = ["L0_attn_a_residual", "L0_attn_a_w_fc", "L0_attn_a_w_proj", "L0_attn_a_ln_g", "L0_attn_a_ln_b",
        "L0_attn_b_Wq", "L0_attn_b_bq", "L0_attn_b_Wk", "L0_attn_b_bk", "L0_attn_b_Wv", "L0_attn_b_bv",
        "L0_attn_b_Wbeta", "L0_attn_b_bbeta", "L0_attn_b_Wo", "L0_attn_b_bo",
        "L0_ffn_W1", "L0_ffn_b1", "L0_ffn_W2", "L0_ffn_b2"]


def kernel(**inputs):
    import numpy as _np
    import concourse.bacc as _bacc
    from concourse import mybir as _mybir
    from concourse.bass_utils import run_bass_kernel_spmd as _run

    nc = _bacc.Bacc("TRN2", target_bir_lowering=False, num_devices=1)
    arrays, args = {}, []
    for name in _INS:
        a = _np.ascontiguousarray(inputs[name])
        arrays[f"in_{name}"] = a
        args.append(nc.dram_tensor(f"in_{name}", a.shape, _mybir.dt.from_np(a.dtype), kind="ExternalInput").ap())
    shape = inputs["L0_attn_a_residual"].shape
    args.append(nc.dram_tensor("out_0", shape, _mybir.dt.float32, kind="ExternalOutput").ap())
    layer_kernel(nc, *args)
    r = _run(nc, [arrays], core_ids=[0])
    return r.results[0]["out_0"]
```

```python
from contextlib import ExitStack

import concourse.bass as bass
from concourse import mybir

ALU = mybir.AluOpType
ACT = mybir.ActivationFunctionType
F32 = mybir.dt.float32
F32R = mybir.dt.float32r
AX_X = mybir.AxisListType.X

P = 128
C = 128
NB = 2
HT = 4
BLK = 8
QT_ = 4
NT = 2
NQ = NT * BLK // QT_
GB = P // NB
NE = 8
FF = 512
FC = FF // P
AH = 4
AD = C // AH
NM = 4
H = 16
D = C // H
R = 2 * D
RV = D
PW = 3 * C + H
HEADS_POOL = range(3, H, 4)
HEADS_SP = [h for h in range(H) if h not in HEADS_POOL]
SEG = 16
EPS = 1e-5
TINY = 1e-18
ROUND = 2.0 ** 23
ROUND_S = 1.5 * 2.0 ** 23


Y_STAGES = ("bias2", "bias2ed", "project", "out", "outed")


def spread(own, other):
    s, other, n_other, filling = [], list(other), len(other), False
    for n, stage in enumerate(own):
        s.append(stage)
        filling = stage[0] in ("down", "mix") or filling and stage[0] not in ("weigh", "mixed")
        while n_other - len(other) < n_other * (n + 1) // len(own):
            if filling and other[0][0] in Y_STAGES:
                break
            s.append(other.pop(0))
            while other and (s[-1][0] in ("bias2", "out")
                             or s[-1][0] == "turn" and s[-1][1] in "PQ" or s[-1][0] == "unfold"):
                s.append(other.pop(0))
    return s + other


def attend(q):
    s = []
    for m in range(NM):
        s += [("score", q, m, h) for h in range(AH)]
        if m:
            s += [("mix", q, m - 1, h) for h in range(AH)]
    return s + [("mix", q, NM - 1, h) for h in range(AH)] + [("mix out", q), ("mix turn", q), ("mixed", q)]


def norm(what, q):
    return [("stats", what, q), ("norm", what, q)]


def turn_x(what, q):
    return [("turn", "x", what, q)]


def route(f):
    return [("route", f), ("turn", "w", f), ("bias2", f), ("bias2ed", f)]


def experts(units, more):
    s, before = [], []
    for unit in units:
        own = []
        for c in range(FC):
            own += [("up", *unit, 2 * c), ("up", *unit, 2 * c + 1)] + before[2 * c:2 * c + 2]
        own += before[2 * FC:]
        before = [("down", *unit, n) for n in range(2 * QT_)] + [("weigh", *unit)]
        s += spread(own, more.get(unit, []))
    return s + before


def passes(*fs):
    return [(f, e) for f in fs for e in range(NE)]


def project(q):
    return [("project", q, i) for i in range(QT_)] + [("lengths", q)]


def blocks(t, half):
    s = [("block", t, j, part) for j in range(half * QT_, (half + 1) * QT_) for part in range(4)]
    return s + [("block", t, BLK, 3)] * half


def transfers(t):
    return ([("turn", "P", t, n) for n in range(2)] + [("unfold", t, n) for n in range(2)]
            + [("turn", "Q", t, n) for n in range(2)] + [("add", t)])


def chain(t):
    return [("state", t, g) for g in range(GB if t == 0 else GB - 1)]


def turn_states(t):
    return [("turn", "S", t, n) for n in range(2)] + [("carry", 0)] * (t == 0)


def read(t, half):
    return [("read", t, j) for j in range(half * QT_, (half + 1) * QT_)]


def put_out(t, half):
    return [("turn", "O", t, half), ("out", t, half), ("outed", t, half)]


def mingle(*lists):
    at = [((n + 0.5) / len(l), k, n) for k, l in enumerate(lists) for n in range(len(l))]
    return [lists[k][n] for _, k, n in sorted(at)]


RECUR = {
    1: (3, 2, 3, 2, 2, 0, 4, 0, 0, 0),
    2: (2, 2, 0, 7, 0, 5, 0, 0, 0, 0),
    3: (0, 4, 8, 1, 4, 0, 0, 0, 0, 0),
    4: (0, 0, 6, 5, 0, 3, 0, 4, 7, 0),
}
CHAIN = {
    2: (0, 0, 0, 0, 0, 0, 0, 2, 9, 15),
    3: (6, 9, 0, 14, 5, 17, 0, 2, 9, 0),
    4: (0, 0, 0, 0, 0, 0, 0, 0, 0, 2),
    5: (0, 0, 0, 17, 12, 10, 17, 14, 7, 0),
    6: (0, 0, 2, 1, 2, 2, 0, 0, 0, 0),
}
NEXT = {
    0: (0, 0, 6, 0, 0, 5, 0, 0, 1, 1),
    1: (0, 0, 5, 0, 0, 0, 1, 0, 1, 2),
    2: (0, 0, 0, 1, 3, 0, 1, 0, 3, 1),
    3: (0, 0, 4, 0, 0, 0, 0, 0, 1, 6),
    4: (0, 0, 0, 2, 0, 0, 0, 1, 4, 0),
    5: (0, 0, 0, 0, 0, 0, 0, 0, 0, 4),
    6: (0, 0, 0, 0, 3, 0, 0, 1, 0, 4),
    7: (0, 0, 0, 2, 0, 0, 0, 0, 0, 0),
}


def plan():
    recur = blocks(0, 0) + blocks(0, 1) + blocks(1, 0) + turn_x("D", 3) + project(3) + [("roots", 3), ("keys", 3)]
    recur += blocks(1, 1)
    steps = []
    for t in range(NT):
        steps += transfers(t) + chain(t) + turn_states(t)
        for half in range(2):
            steps += read(t, half) + put_out(t, half)
    ahead = [("split", e) for e in range(4, NE)] + route(0)
    for q in range(1, NQ):
        ahead += norm("Y", q) + norm("Z", q) + turn_x("Z", q) + route(q)
    for f in range(NQ, 2 * NQ):
        ahead += norm("F", f) + turn_x("F", f) + route(f)
    lists = ((RECUR, recur), (CHAIN, steps), (NEXT, ahead))

    def taken(stages, n):
        out = stages[:n]
        del stages[:n]
        return out

    def others(f, part):
        return [taken(stages, counts[f][part]) for counts, stages in lists if f in counts]

    def attended(q):
        a = attend(q)
        s = []
        if q == 0:
            s += taken(a, 16) + [("split", e) for e in range(4)]
        if q:
            s += norm("D", q - 1) + taken(a, 4) + turn_x("D", q - 1) + project(q - 1)
            inner = taken(a, 14)
            s += inner[:4] + [("roots", q - 1), ("keys", q - 1)] + mingle(inner[4:], *others(q, 0))
            s += mingle(taken(a, 12), *others(q, 1))
        return s + a + norm("F", q) + turn_x("F", q)

    def units(*fs):
        return experts(passes(*fs), {(f, e): mingle(*others(f, 2 + e)) for f in fs for e in range(NE)})

    s = norm("Y", 0) + norm("Z", 0) + turn_x("Z", 0)
    for q in range(NQ):
        s += attended(q) + units(q)
    return s + norm("D", NQ - 1) + units(*range(NQ, 2 * NQ))


def layer_kernel(nc, residual, w_fc, w_proj, ln_g, ln_b, Wq, bq, Wk, bk, Wv, bv, Wbeta, bbeta, Wo, bo,
                 W1, b1, W2, b2, out):
    stages = plan()

    def order(*kinds):
        return {s: n for n, s in enumerate(x for x in stages if x[0] in kinds)}

    norm_no = order("norm")
    turn_no = order("turn")
    y_no = {}
    for s in stages:
        if s[0] == "mix" and s[2] == s[3] == 0:
            y_no["mix", s[1]] = len(y_no)
        elif s[0] == "mix turn":
            y_no[s] = len(y_no)
        elif s[0] in ("bias2", "project", "out"):
            y_no[s] = len(y_no)
        elif s[0] == "down" and s[3] == 0:
            y_no["down", s[1], s[2]] = len(y_no)
    z_no = {s: n for n, s in enumerate(s for s in stages if s[0] == "score" or s[0] == "up" and s[3] % 2 == 0)}
    state_no, read_no = order("state"), order("read")

    with ExitStack() as ctx:
        def sb(name, shape, dtype=F32):
            return ctx.enter_context(nc.sbuf_tensor(name, [P, *shape], dtype))

        def bank(name):
            return ctx.enter_context(nc.psum_tensor(name, [P, 512], F32))

        def sem(name):
            return ctx.enter_context(nc.semaphore(name))

        X = sb("X", [NB * BLK, C])
        w1_hi = sb("w1_hi", [NE, FF], F32R)
        w1_lo = sb("w1_lo", [NE, FF], F32R)
        w2 = sb("w2", [NE, FC, C])
        b1_cols = sb("b1_cols", [NE * FC])
        b2_rows = sb("b2_rows", [C])
        table_k = sb("table_k", [NM, AH, P])
        table_v = sb("table_v", [NM, AD])
        gain = sb("gain", [1])
        shift = sb("shift", [1])
        w_in = sb("w_in", [PW])
        b_in = sb("b_in", [PW])
        w_out = sb("w_out", [C])
        b_out = sb("b_out", [C])
        ones = sb("ones", [P])
        ident = sb("ident", [P])
        numbers = sb("numbers", [NE])
        halves = sb("halves", [QT_])
        stat = sb("stat", [2, QT_, 6])
        mv = sb("mv", [2, QT_, 2])
        var_eps = sb("var_eps", [2, QT_])
        rstd = sb("rstd", [2, QT_])
        YN = sb("YN", [4, QT_, C])
        zT = sb("zT", [2, QT_ * P])
        dT = sb("dT", [QT_ * P])
        xT = sb("xT", [QT_ * P])
        xT_hi = sb("xT_hi", [2, QT_ * P], F32R)
        xT_lo = sb("xT_lo", [2, QT_ * P], F32R)
        rt = sb("rt", [8, QT_])
        hit = sb("hit", [QT_, NE])
        wt = sb("wt", [4, QT_, NE])
        wT = sb("wT", [2, QT_ * P])
        hid = sb("hid", [2, 4, 512])
        mixT = sb("mixT", [QT_ * P])
        qkvb = sb("qkvb", [BLK, PW])
        nkb = sb("nkb", [BLK, C])
        beta = sb("beta", [QT_, H])
        kn = sb("kn", [3, QT_, H])
        M = sb("M", [R, H, D])
        tmp = sb("tmp", [R, H, D])
        by_q = sb("by_q", [R, H, D])
        dl = sb("dl", [R, H])
        res = sb("res", [NB, BLK, R, H])
        pT = sb("pT", [D, P])
        qT = sb("qT", [D, P])
        first = sb("first", [NB, D])
        unfolded = sb("unfolded", [2, HT, D, NB, SEG])
        ST = sb("ST", [D, P])
        S = sb("S", [D, H, D])
        O = sb("O", [BLK, H, D])
        early = M[:, :, :, :].rearrange("p r h e -> p (r h e)")
        wfc, wproj, b1_rows = (early[:, i * C:(i + 1) * C] for i in range(3))
        w1 = res[:, :, :, :, :].rearrange("p b j r h -> p (b j r h)").rearrange("p (e f) -> p e f", e=NE)
        wfc4 = early[:, 3 * C:(3 + NM) * C].rearrange("p (m h d) -> p m h d", m=NM, h=AH)
        by_back = table_k[:, 0:2, :, :].rearrange("p m h r -> p (m h r)")\
            .rearrange("p (d h e) -> p d h e", d=D, h=H)
        oT = pT

        TB = [bank(f"TB{i}") for i in range(2)]
        ZB = [bank(f"ZB{i}") for i in range(2)]
        YB = [bank(f"YB{i}") for i in range(2)]
        CB = ctx.enter_context(nc.psum_tensor("CB", [P, NB, GB, D], F32))

        x_in = [sem(f"x_in{q}") for q in range(NQ)]
        consts_in = sem("consts_in")
        w_in_in = sem("w_in_in")
        w1_in = [sem(f"w1_in{e}") for e in range(NE)]
        w2_in = sem("w2_in")
        w1_hi_ready = sem("w1_hi_ready")
        w1_split = sem("w1_split")
        xT_hi_ready = sem("xT_hi_ready")
        xT_lo_ready = sem("xT_lo_ready")
        pool_consts = sem("pool_consts")
        ident_ready = sem("ident_ready")
        var_ready = sem("var_ready")
        eps_added = sem("eps_added")
        rstd_ready = sem("rstd_ready")
        norm_ready = sem("norm_ready")
        wfc4_ready = sem("wfc4_ready")
        turn_full = sem("turn_full")
        turn_used = sem("turn_used")
        z_full = sem("z_full")
        z_used = sem("z_used")
        squared = sem("squared")
        y_full = sem("y_full")
        y_used = sem("y_used")
        route_ready = sem("route_ready")
        keys_ready = sem("keys_ready")
        length2_ready = sem("length2_ready")
        roots_ready = sem("roots_ready")
        m_ready = sem("m_ready")
        m_ready_pool = sem("m_ready_pool")
        dl_ready = sem("dl_ready")
        outer_ready = sem("outer_ready")
        by_q_ready = sem("by_q_ready")
        res_ready = sem("res_ready")
        s_by_q_ready = sem("s_by_q_ready")
        unfold_zeroed = sem("unfold_zeroed")
        unfold_in = [sem(f"unfold_in{i}") for i in range(2)]
        unfold_in_pool = [sem(f"unfold_in_pool{i}") for i in range(2)]
        state_full = sem("state_full")
        state_ready = sem("state_ready")
        o_ready = sem("o_ready")
        stored = sem("stored")
        dve_done = sem("dve_done")

        N_SMALL = 7

        def quad(t, q):
            return t[:, q * QT_:(q + 1) * QT_, :]

        def flat(ap):
            return ap.rearrange("p a b -> p (a b)")

        def x_dram(a, q, b):
            t, half = divmod(q, 2)
            return a[b].rearrange("(t g j) c -> t g j c", t=NT, j=BLK)[t, :, half * QT_:(half + 1) * QT_, :]

        def x_rows(q, b):
            return X[b * GB:(b + 1) * GB, q * QT_:(q + 1) * QT_, :]

        def turned(s):
            return 2 + turn_no[s] + 1

        def by_pool(t, j):
            return t == NT - 1 and j % 2 == 1

        def s_by_q(j):
            half = j // 2 % 2
            return by_q[:, half * D:(half + 1) * D, :, :]

        def back(t, j):
            return res[:, t, j, D:R, :].rearrange("p e (o h) -> p o h e", o=1).to_broadcast([P, D, H, D])

        def updates(t, j):
            return t * (BLK - 1) + j

        def unfold(engine, done, t, seg, heads):
            n = t * (GB // SEG) + seg
            if n >= 2:
                was, part = divmod(n - 2, GB // SEG)
                last = min((part + 1) * SEG, GB if was == 0 else GB - 1) - 1
                engine.wait_ge(state_full, state_no["state", was, last] + 1)
            engine.wait_ge(turn_used, turned(("turn", "P", t, 1)))
            for h in heads:
                engine.dma_start(unfolded[h * D:(h + 1) * D, n % 2, h % HT, :, :, :],
                                 pT[h:P:H, :, :].rearrange("x e (b g) -> x e b g", b=NB)
                                 [:, :, :, seg * SEG:(seg + 1) * SEG]).then_inc(done[n % 2], 16)

        block = ctx.enter_context(nc.Block())

        @block.sync
        def _(sp):
            for b in range(NB):
                sp.dma_start(x_rows(0, b), x_dram(residual, 0, b)).then_inc(x_in[0], 16)
            sp.dma_start(wfc, w_fc).then_inc(consts_in, 16)
            sp.dma_start(wproj, w_proj).then_inc(consts_in, 16)
            sp.dma_start(gain[:, :], ln_g.rearrange("(c o) -> c o", o=1)).then_inc(consts_in, 16)
            sp.dma_start(shift[:, :], ln_b.rearrange("(c o) -> c o", o=1)).then_inc(consts_in, 16)
            sp.dma_start(b1_rows[0:NE * FC, :], b1.rearrange("e (c p) -> (e c) p", p=P)).then_inc(consts_in, 16)
            sp.dma_start(b2_rows[0:NE, :], b2).then_inc(consts_in, 16)
            sp.dma_start(b_out[0:1, :], bo.rearrange("(o c) -> o c", o=1)).then_inc(consts_in, 16)
            for q in range(1, NQ):
                for b in range(NB):
                    sp.dma_start(x_rows(q, b), x_dram(residual, q, b)).then_inc(x_in[q], 16)
            for e in range(NE):
                sp.dma_start(w1[:, e, :], W1[e]).then_inc(w1_in[e], 16)
            for e in range(NE):
                sp.dma_start(w2[:, e, :, :], W2[e].rearrange("(c p) d -> p c d", p=P)).then_inc(w2_in, 16)
            at = 0
            for w, bias in ((Wq, bq), (Wk, bk), (Wv, bv), (Wbeta, bbeta)):
                n = w.shape[1]
                sp.dma_start(w_in[:, at:at + n], w).then_inc(w_in_in, 16)
                sp.dma_start(b_in[:, at:at + n],
                             bias.rearrange("(o c) -> o c", o=1).broadcast_to([P, n])).then_inc(w_in_in, 16)
                at += n
            sp.dma_start(w_out[:, :], Wo).then_inc(w_in_in, 16)

            sp.wait_ge(unfold_zeroed, 1)
            for s in stages:
                if s[0] == "unfold":
                    unfold(sp, unfold_in, s[1], s[2], HEADS_SP)
                elif s[0] == "state" and s[2] in (SEG, 2 * SEG):
                    unfold(sp, unfold_in, s[1], s[2] // SEG + 1, HEADS_SP)
            for q in range(NQ):
                sp.wait_ge(y_used, y_no["down", NQ + q, NE - 1] + 1)
                for b in range(NB):
                    sp.dma_start(x_dram(out, q, b), x_rows(q, b)).then_inc(stored, 16)
            sp.wait_ge(stored, 16 * NQ * NB)

        @block.gpsimd
        def _(pool):
            pool.memset(ident[:, :], 1.0).then_inc(pool_consts, 1)
            pool.wait_ge(pool_consts, 1)
            pool.affine_select(out=ident[:, :], in_=ident[:, :], compare_op=ALU.is_equal, fill=0.0, base=0,
                               pattern=[[-1, P]], channel_multiplier=1).then_inc(ident_ready, 1)
            pool.memset(halves[:, :], -0.5).then_inc(pool_consts, 1)
            pool.wait_ge(pool_consts, 2)
            pool.memset(ones[:, :], 1.0)
            pool.iota(numbers[:, :], pattern=[[1, NE]], base=0, channel_multiplier=0,
                      allow_small_or_imprecise_dtypes=True)
            pool.memset(ST[:, :, 0:P:GB], 0.0).then_inc(pool_consts, 1)
            unfold_set = False
            for s in stages:
                if s[0] == "stats":
                    n = norm_no["norm", s[1], s[2]]
                    pool.wait_ge(var_ready, n + 1)
                    pool.tensor_scalar(var_eps[:, n % 2, :], mv[:, n % 2, :, 1], EPS, 1.0, ALU.add,
                                       ALU.mult).then_inc(eps_added, 1)
                    pool.wait_ge(eps_added, n + 1)
                    pool.tensor_tensor(rstd[:, n % 2, :], var_eps[:, n % 2, :], halves[:, 0:QT_],
                                       ALU.pow).then_inc(rstd_ready, 1)
                elif s[0] == "block" and s[2] < BLK and s[3] >= 2:
                    b, j, part = s[1:]
                    n = b * BLK + j
                    if part == 2 and j:
                        pool.wait_ge(dl_ready, updates(b, j))
                        pool.tensor_tensor(tmp[:, RV:R, :, :],
                                           dl[:, RV:R, :].rearrange("p r (h o) -> p r h o", o=1)
                                           .to_broadcast([P, R - RV, H, D]),
                                           nkb[:, j, :].rearrange("p (o h e) -> p o h e", o=1, h=H)
                                           .to_broadcast([P, R - RV, H, D]), ALU.mult).then_inc(outer_ready, 1)
                    elif part == 3:
                        if j:
                            pool.wait_ge(by_q_ready, n)
                            pool.wait_ge(outer_ready, updates(b, j))
                            pool.tensor_tensor(M[:, RV:R, :, :], M[:, RV:R, :, :], tmp[:, RV:R, :, :],
                                               ALU.add).then_inc(m_ready_pool, 1)
                            pool.wait_ge(m_ready_pool, updates(b, j))
                        pool.wait_ge(m_ready, n + 1)
                        if n:
                            pool.wait_ge(res_ready, n)
                        pool.tensor_tensor(by_q[:, :, :, :].rearrange("p r h e -> p r (h e)"),
                                           M[:, :, :, :].rearrange("p r h e -> p r (h e)"),
                                           qkvb[:, j, 0:C].rearrange("p (o c) -> p o c", o=1)
                                           .to_broadcast([P, R, C]), ALU.mult).then_inc(by_q_ready, 1)
                elif s[0] == "turn" and s[1:3] == ("x", "F"):
                    f = s[3]
                    pool.wait_ge(xT_hi_ready, f + 1)
                    pool.wait_ge(turn_used, turned(s))
                    pool.tensor_tensor(xT_lo[:, f % 2, :], xT[:, :], xT_hi[:, f % 2, :], ALU.subtract)\
                        .then_inc(xT_lo_ready, 1)
                elif s[0] == "read" and by_pool(s[1], s[2]):
                    b, j = s[1:]
                    pool.wait_ge(turn_used, turned(("turn", "S", b, 1)))
                    pool.wait_ge(res_ready, NT * BLK)
                    if j > 3:
                        pool.wait_ge(o_ready, read_no["read", b, j - 4] + 1)
                    pool.tensor_tensor(s_by_q(j), S[:, :, :, :], back(b, j), ALU.mult).then_inc(s_by_q_ready, 1)
                elif s[0] == "unfold":
                    unfold(pool, unfold_in_pool, s[1], s[2], HEADS_POOL)
                elif s[0] == "state" and s[2] in (SEG, 2 * SEG):
                    unfold(pool, unfold_in_pool, s[1], s[2] // SEG + 1, HEADS_POOL)
                if not unfold_set and s[0] == "up":
                    unfold_set = True
                    pool.memset(unfolded[:, :, :, :, :, :], 0.0).then_inc(unfold_zeroed, 1)

        @block.tensor
        def _(pe):
            fills = [0]

            def turn(parts, n, normed=None):
                bank_ = TB[n % 2]
                if n >= 2:
                    pe.wait_ge(turn_used, n - 1)
                for i, (at, ap, rows, cols) in enumerate(parts):
                    if normed is not None:
                        pe.wait_ge(norm_ready, normed + i + 1)
                    last = pe.transpose(bank_[0:rows, at:at + cols], ap, ident[0:cols, 0:cols])
                last.then_inc(turn_full, 1)

            def y_bank(key):
                n = y_no[key]
                if n >= 2:
                    pe.wait_ge(y_used, n - 1)
                return YB[n % 2]

            pe.wait_ge(ident_ready, 1)
            pe.wait_ge(consts_in, 16 * N_SMALL)
            pe.wait_ge(wfc4_ready, 1)
            turn([(m * P, flat(wfc4[:, m, :, :]), P, P) for m in range(NM)], 0)
            turn([(0, wproj, P, P), (P, b1_rows[0:NE * FC, :], P, NE * FC)], 1)
            pe.wait_ge(pool_consts, 3)
            unfolds = 0
            for s in stages:
                kind = s[0]
                if kind == "turn":
                    n = 2 + turn_no[s]
                    what = s[1]
                    if what == "x":
                        k = norm_no["norm", s[2], s[3]]
                        turn([(i * P, YN[:, k % 4, i, :], P, P) for i in range(QT_)], n, QT_ * k)
                    elif what == "w":
                        pe.wait_ge(route_ready, s[2] + 1)
                        turn([(i * P, wt[:, s[2] % 4, i, :], NE, P) for i in range(QT_)], n)
                    elif what == "P":
                        pe.wait_ge(m_ready, BLK * (s[2] + 1))
                        pe.wait_ge(m_ready_pool, updates(s[2], BLK - 1))
                        turn([(i * P, flat(M[:, D:R, :, 4 * s[3] + i]), P, P) for i in range(4)], n)
                    elif what == "Q":
                        pe.wait_ge(m_ready, BLK * (s[2] + 1))
                        pe.wait_ge(m_ready_pool, updates(s[2], BLK - 1))
                        turn([(i * P, flat(M[:, 4 * s[3] + i, :, :]), P, P) for i in range(4)], n)
                    elif what == "S":
                        pe.wait_ge(state_ready, GB if s[2] == 0 else 2 * GB)
                        turn([(i * P, ST[:, 4 * s[3] + i, :], P, P) for i in range(4)], n)
                    elif what == "O":
                        pe.wait_ge(o_ready, read_no["read", s[2], 4 * s[3] + 3] + 1)
                        turn([(i * P, O[:, 4 * s[3] + i, :, :].rearrange("p h d -> p (h d)"), P, P)
                              for i in range(4)], n)
                elif kind == "score":
                    q, m, h = s[1:]
                    if h == m == 0:
                        pe.wait_ge(turn_used, turned(("turn", "x", "Z", q)))
                    z = z_no[s]
                    if z >= 2:
                        pe.wait_ge(z_used, z - 1)
                    pe.matmul(ZB[z % 2][:, :], table_k[:, m, h, :], zT[:, q % 2, :], start=True,
                              stop=True).then_inc(z_full, 1)
                elif kind == "mix":
                    q, m, h = s[1:]
                    if h == m == 0:
                        y_bank(("mix", q))
                    if h == 0:
                        pe.wait_ge(squared, AH * (q * NM + m + 1))
                    last = pe.matmul(YB[y_no["mix", q] % 2][h * AD:(h + 1) * AD, :], table_v[:, m, :],
                                     hid[:, (q * NM + m) % 2, h, :], start=(m == 0), stop=(m == NM - 1),
                                     skip_group_check=True)
                    if h == AH - 1 and m == NM - 1:
                        last.then_inc(y_full, 1)
                elif kind == "mix turn":
                    pe.wait_ge(y_used, y_no["mix", s[1]] + 1)
                    yb = y_bank(s)
                    for i in range(QT_):
                        last = pe.transpose(yb[:, i * P:(i + 1) * P], mixT[:, i * P:(i + 1) * P], ident[:, :])
                    last.then_inc(y_full, 1)
                elif kind == "bias2":
                    f = s[1]
                    pe.wait_ge(turn_used, turned(("turn", "w", f)))
                    yb = y_bank(s)
                    for i in range(QT_):
                        last = pe.matmul(yb[:, i * C:(i + 1) * C], wT[0:NE, f % 2, i * P:(i + 1) * P],
                                         b2_rows[0:NE, :], start=True, stop=True)
                    last.then_inc(y_full, 1)
                elif kind == "up":
                    f, e, n = s[1:]
                    c, half = divmod(n, 2)
                    cols = slice(c * P, (c + 1) * P)
                    if c == 0 and half == 0:
                        if f == 0:
                            pe.wait_ge(w1_split, e + 1)
                        pe.wait_ge(xT_hi_ready, f + 1)
                    if c == 0 and half:
                        pe.wait_ge(xT_lo_ready, f + 1)
                    z = z_no["up", f, e, 2 * c]
                    zb = ZB[z % 2][:, :]
                    if not half:
                        if z >= 2:
                            pe.wait_ge(z_used, z - 1)
                        pe.matmul(zb, w1_hi[:, e, cols], xT_hi[:, f % 2, :], start=True, stop=False)
                        pe.matmul(zb, w1_lo[:, e, cols], xT_hi[:, f % 2, :], start=False, stop=False)
                    else:
                        pe.matmul(zb, w1_hi[:, e, cols], xT_lo[:, f % 2, :], start=False, stop=True)\
                          .then_inc(z_full, 1)
                elif kind == "down":
                    f, e, n = s[1:]
                    i, half = divmod(n, 2)
                    u = f * NE + e
                    if n == 0:
                        if f == e == 0:
                            pe.wait_ge(w2_in, 16 * NE)
                        y_bank(("down", f, e))
                        pe.wait_ge(z_used, z_no["up", f, e, 2 * FC - 2] + 1)
                    yb = YB[y_no["down", f, e] % 2]
                    for c in range(half * FC // 2, (half + 1) * FC // 2):
                        last = pe.matmul(yb[:, i * C:(i + 1) * C], hid[:, u % 2, c, i * P:(i + 1) * P],
                                         w2[:, e, c, :], start=(c == 0), stop=(c == FC - 1))
                    if n == 2 * QT_ - 1:
                        last.then_inc(y_full, 1)
                elif kind == "project":
                    q, i = s[1:]
                    if i == 0:
                        pe.wait_ge(w_in_in, 16 * 9)
                        pe.wait_ge(turn_used, turned(("turn", "x", "D", q)))
                    pe.matmul(y_bank(s)[:, 0:PW], dT[:, i * P:(i + 1) * P], w_in[:, :], start=True,
                              stop=True).then_inc(y_full, 1)
                elif kind == "add":
                    t = s[1]
                    pe.wait_ge(turn_used, turned(("turn", "Q", t, 1)))
                    if t:
                        pe.wait_ge(state_ready, GB)
                    for b in range(NB):
                        pe.matmul(CB[:, b, :, :], ident[:, :],
                                  qT[:, :, b * GB:(b + 1) * GB].rearrange("p d g -> p g d"),
                                  start=True, stop=True)
                elif kind == "state":
                    t, g = s[1:]
                    n = t * (GB // SEG) + g // SEG
                    if g % SEG == 0:
                        pe.wait_ge(unfold_in[n % 2], 16 * len(HEADS_SP) * (n // 2 + 1))
                        pe.wait_ge(unfold_in_pool[n % 2], 16 * len(HEADS_POOL) * (n // 2 + 1))
                    if t or g:
                        pe.wait_ge(state_ready, t * (GB + 1) + g)
                    for b in range(NB):
                        for at in range(0, P, HT * D):
                            rows = slice(at, at + HT * D)
                            last = pe.matmul(CB[rows, b, g, :],
                                             unfolded[rows, n % 2, :, :, b, g % SEG].rearrange("p h e -> p (h e)"),
                                             ST[rows, :, b * GB + g], start=False, stop=True,
                                             skip_group_check=True)
                    last.then_inc(state_full, 1)
                elif kind == "out":
                    b, n = s[1:]
                    pe.wait_ge(turn_used, turned(("turn", "O", b, n)))
                    yb = y_bank(s)
                    for i in range(QT_):
                        pe.matmul(yb[:, i * C:(i + 1) * C], ones[0:1, :], b_out[0:1, :], start=True, stop=False)
                        last = pe.matmul(yb[:, i * C:(i + 1) * C], oT[:, n * QT_ + i, :], w_out[:, :],
                                         start=False, stop=True)
                    last.then_inc(y_full, 1)

        @block.scalar
        def _(act):
            act.wait_ge(wfc4_ready, 1)
            act.wait_ge(turn_full, 1)
            for h in range(AH):
                rows = slice(h * AD, (h + 1) * AD)
                last = act.activation(table_k[rows, :, h, :], TB[0][rows, :].rearrange("p (m c) -> p m c", m=NM),
                                      ACT.Copy)
            last.then_inc(turn_used, 1)
            act.wait_ge(turn_full, 2)
            act.activation(table_v[:, :, :], TB[1][:, 0:C].rearrange("p (m d) -> p m d", m=NM), ACT.Copy)
            act.activation(b1_cols[:, :], TB[1][:, P:P + NE * FC], ACT.Copy).then_inc(turn_used, 1)
            for s in stages:
                kind = s[0]
                if kind == "turn":
                    n = 2 + turn_no[s]
                    act.wait_ge(turn_full, n + 1)
                    tb = TB[n % 2]
                    four = tb[:, :].rearrange("p (i t) -> p i t", i=4)
                    what = s[1]
                    if what == "x" and s[2] == "Z":
                        act.wait_ge(consts_in, 16 * N_SMALL)
                        ins = act.activation(zT[:, s[3] % 2, :], tb[:, :], ACT.Identity, bias=shift[:, 0:1],
                                             scale=gain[:, 0:1])
                    elif what == "x" and s[2] == "F":
                        f = s[3]
                        if f:
                            act.wait_ge(xT_lo_ready, f)
                        act.activation(xT_hi[:, f % 2, :], tb[:, :], ACT.Copy).then_inc(xT_hi_ready, 1)
                        ins = act.activation(xT[:, :], tb[:, :], ACT.Copy)
                    elif what == "x":
                        ins = act.activation(dT[:, :], tb[:, :], ACT.Copy)
                    elif what == "w":
                        ins = act.activation(wT[0:NE, s[2] % 2, :], tb[0:NE, :], ACT.Copy)
                    elif what == "P":
                        ins = act.activation(pT[:, 4 * s[3]:4 * s[3] + 4, :], four, ACT.Copy)
                    elif what == "Q":
                        ins = act.activation(qT[:, 4 * s[3]:4 * s[3] + 4, :], four, ACT.Copy)
                    elif what == "S":
                        ins = act.activation(S[:, 4 * s[3]:4 * s[3] + 4, :, :],
                                             tb[:, :].rearrange("p (d h e) -> p d h e", d=4, h=H), ACT.Copy)
                    elif what == "O":
                        ins = act.activation(oT[:, 4 * s[3]:4 * s[3] + 4, :], four, ACT.Copy)
                    ins.then_inc(turn_used, 1)
                elif kind == "score":
                    q, m, h = s[1:]
                    z = z_no[s]
                    n = m * AH + h
                    act.wait_ge(z_full, z + 1)
                    act.activation(hid[:, (q * NM + m) % 2, h, :], ZB[z % 2][:, :], ACT.Relu).then_inc(z_used, 1)
                    for d in range(max(n - 1, 0), n + (n == NM * AH - 1)):
                        act.wait_ge(z_used, z + 1 + d - n)
                        sq = hid[:, (q * NM + d // AH) % 2, d % AH, :]
                        act.activation(sq, sq, ACT.Square).then_inc(squared, 1)
                elif kind == "up" and s[3] % 2:
                    f, e, c = s[1], s[2], s[3] // 2
                    u = f * NE + e
                    z = z_no["up", f, e, 2 * c]
                    act.wait_ge(z_full, z + 1)
                    n = e * FC + c
                    act.activation(hid[:, u % 2, c, :], ZB[z % 2][:, :], ACT.Relu,
                                   bias=b1_cols[:, n:n + 1]).then_inc(z_used, 1)
                elif kind == "roots":
                    q = s[1]
                    if q:
                        act.wait_ge(keys_ready, q)
                    act.wait_ge(length2_ready, q + 1)
                    js = slice((q % 2) * QT_, (q % 2 + 1) * QT_)
                    if q % 2:
                        act.activation(kn[:, 1, :, :], kn[:, 0, :, :], ACT.Sqrt)
                        act.activation(beta[:, :, :], qkvb[:, js, 3 * C:PW], ACT.Sigmoid).then_inc(roots_ready, 1)
                    else:
                        act.activation(beta[:, :, :], qkvb[:, js, 3 * C:PW], ACT.Sigmoid)
                        act.activation(kn[:, 1, :, :], kn[:, 0, :, :], ACT.Sqrt).then_inc(roots_ready, 1)
                elif kind == "state":
                    t, g = s[1:]
                    act.wait_ge(state_full, state_no[s] + 1)
                    to = ST[:, :, g + 1:P:GB].rearrange("p d b -> p b d") if g < GB - 1 else first[:, :, :]
                    act.activation(to, CB[:, :, g, :], ACT.Copy).then_inc(state_ready, 1)
                elif kind == "carry":
                    act.wait_ge(turn_full, 2 + turn_no["turn", "S", 0, 1] + 1)
                    act.wait_ge(state_ready, GB)
                    act.activation(ST[:, :, 0:P:GB].rearrange("p d b -> p b d"), first[:, :, :], ACT.Copy)\
                       .then_inc(state_ready, 1)

        @block.vector
        def _(dve):
            links = [0]

            def link(ins):
                links[0] += 1
                ins.then_inc(dve_done, 1)
                dve.wait_ge(dve_done, links[0])

            dve.memset(table_k[:, :, :, :], 0.0)
            for s in stages:
                kind = s[0]
                if s == ("norm", "Y", 0):
                    dve.wait_ge(consts_in, 16 * N_SMALL)
                    for m in range(NM):
                        last = dve.tensor_copy(wfc4[:, m, :, :], wfc[:, m * AD:(m + 1) * AD]
                                               .rearrange("p (o d) -> p o d", o=1).to_broadcast([P, AH, AD]))
                    last.then_inc(wfc4_ready, 1)
                elif s == ("route", 0):
                    dve.wait_ge(pool_consts, 3)
                if kind == "stats":
                    what, q = s[1:]
                    n = norm_no["norm", what, q]
                    if what == "Y":
                        dve.wait_ge(x_in[q], 16 * NB)
                    src = YN[:, norm_no["norm", "Y", q] % 4, :, :] if what == "Z" else quad(X, q % NQ)
                    for i in range(QT_):
                        last = dve.bn_stats(stat[:, n % 2, i, :], src[:, i, :])
                    link(last)
                    for i in range(QT_):
                        last = dve.bn_aggr(mv[:, n % 2, i, :], stat[:, n % 2, i, :])
                    last.then_inc(var_ready, 1)
                elif kind == "norm":
                    what, q = s[1:]
                    n = norm_no[s]
                    src = YN[:, norm_no["norm", "Y", q] % 4, :, :] if what == "Z" else quad(X, q % NQ)
                    dve.wait_ge(rstd_ready, n + 1)
                    old = [t for t in turn_no if t[1] == "x" and norm_no["norm", t[2], t[3]] == n - 4]
                    if old:
                        dve.wait_ge(turn_full, 2 + turn_no[old[0]] + 1)
                    for i in range(QT_):
                        dve.tensor_scalar(YN[:, n % 4, i, :], src[:, i, :], mv[:, n % 2, i, 0:1],
                                          rstd[:, n % 2, i:i + 1], ALU.subtract, ALU.mult).then_inc(norm_ready, 1)
                    dve.wait_ge(norm_ready, QT_ * (n + 1))
                    if what == "Y":
                        link(dve.tensor_tensor(flat(quad(X, q)), flat(quad(X, q)), flat(YN[:, n % 4, :, :]),
                                               ALU.add))
                elif kind == "split":
                    e = s[1]
                    dve.wait_ge(w1_in[e], 16)
                    dve.tensor_copy(w1_hi[:, e, :], w1[:, e, :]).then_inc(w1_hi_ready, 1)
                    dve.wait_ge(w1_hi_ready, e + 1)
                    dve.tensor_tensor(w1_lo[:, e, :], w1[:, e, :], w1_hi[:, e, :], ALU.subtract)\
                       .then_inc(w1_split, 1)
                    dve.wait_ge(w1_split, e + 1)
                elif kind == "mix out":
                    y = y_no["mix", s[1]]
                    dve.wait_ge(y_full, y + 1)
                    dve.tensor_copy(mixT[:, :], YB[y % 2][:, :]).then_inc(y_used, 1)
                    dve.wait_ge(y_used, y + 1)
                elif kind in ("mixed", "bias2ed", "outed"):
                    if kind == "mixed":
                        y, q = y_no["mix turn", s[1]], s[1]
                    elif kind == "bias2ed":
                        y, q = y_no["bias2", s[1]], s[1] % NQ
                    else:
                        y, q = y_no["out", s[1], s[2]], 2 * s[1] + s[2]
                    dve.wait_ge(y_full, y + 1)
                    link_to = dve.tensor_tensor(flat(quad(X, q)), flat(quad(X, q)), YB[y % 2][:, :], ALU.add)
                    link_to.then_inc(y_used, 1)
                    dve.wait_ge(y_used, y + 1)
                elif kind == "route":
                    f = s[1]
                    y = YN[:, norm_no["norm", "F", f] % 4, :, :]
                    sm, ab, rd, up_, fl, ng, t8, hh = (rt[:, i, :] for i in range(8))
                    link(dve.tensor_tensor(sm, y[:, :, 0], y[:, :, 1], ALU.add))
                    link(dve.scalar_tensor_tensor(out=ab, in0=sm, scalar=-1.0, in1=sm, op0=ALU.mult, op1=ALU.max))
                    link(dve.tensor_scalar(rd, ab, ROUND, None, ALU.add))
                    link(dve.tensor_scalar(rd, rd, ROUND, None, ALU.subtract))
                    link(dve.tensor_tensor(up_, rd, ab, ALU.is_gt))
                    link(dve.tensor_tensor(fl, rd, up_, ALU.subtract))
                    link(dve.tensor_scalar(ng, sm, 0.0, -2.0, ALU.is_lt, ALU.mult))
                    link(dve.scalar_tensor_tensor(out=hh, in0=ng, scalar=1.0, in1=fl, op0=ALU.add, op1=ALU.mult))
                    link(dve.tensor_scalar(t8, hh, 1.0 / NE, None, ALU.mult))
                    link(dve.tensor_scalar(rd, t8, ROUND_S, None, ALU.add))
                    link(dve.tensor_scalar(rd, rd, ROUND_S, None, ALU.subtract))
                    link(dve.tensor_tensor(up_, rd, t8, ALU.is_gt))
                    link(dve.tensor_tensor(fl, rd, up_, ALU.subtract))
                    link(dve.scalar_tensor_tensor(out=hh, in0=fl, scalar=-float(NE), in1=hh, op0=ALU.mult,
                                                  op1=ALU.add))
                    link(dve.tensor_tensor(hit[:, :, :],
                                           hh.rearrange("p (i o) -> p i o", o=1).to_broadcast([P, QT_, NE]),
                                           numbers[:, :].rearrange("p (o e) -> p o e", o=1)
                                           .to_broadcast([P, QT_, NE]), ALU.is_equal))
                    w = wt[:, f % 4, :, :]
                    link(dve.tensor_scalar(hit[:, :, :], hit[:, :, :], 0.5, None, ALU.mult))
                    if f >= 4:
                        dve.wait_ge(turn_full, 2 + turn_no["turn", "w", f - 4] + 1)
                    dve.tensor_tensor(w[:, :, 1:NE], hit[:, :, 1:NE], hit[:, :, 0:NE - 1], ALU.add)
                    dve.tensor_tensor(w[:, :, 0:1], hit[:, :, 0:1], hit[:, :, NE - 1:NE], ALU.add)\
                       .then_inc(route_ready, 1)
                    dve.wait_ge(route_ready, f + 1)
                elif kind == "weigh":
                    f, e = s[1:]
                    y = y_no["down", f, e]
                    dve.wait_ge(y_full, y + 1)
                    for i in range(QT_):
                        xq = X[:, (f % NQ) * QT_ + i, :]
                        last = dve.scalar_tensor_tensor(out=xq, in0=YB[y % 2][:, i * C:(i + 1) * C],
                                                        scalar=wt[:, f % 4, i, e:e + 1], in1=xq, op0=ALU.mult,
                                                        op1=ALU.add)
                    last.then_inc(y_used, 1)
                    dve.wait_ge(y_used, y + 1)
                elif kind == "project":
                    q, i = s[1:]
                    y = y_no[s]
                    dve.wait_ge(y_full, y + 1)
                    dve.tensor_tensor(qkvb[:, (q % 2) * QT_ + i, :], YB[y % 2][:, 0:PW], b_in[:, :], ALU.add)\
                       .then_inc(y_used, 1)
                    dve.wait_ge(y_used, y + 1)
                elif kind == "lengths":
                    q = s[1]
                    js = slice((q % 2) * QT_, (q % 2 + 1) * QT_)
                    k3 = qkvb[:, js, C:2 * C]
                    t4 = mixT[:, :]
                    link(dve.tensor_tensor(t4.rearrange("p (j c) -> p j c", j=QT_), k3, k3, ALU.mult))
                    dve.tensor_reduce(flat(kn[:, 0, :, :]), t4.rearrange("p (a e) -> p a e", e=D), AX_X, ALU.add)\
                       .then_inc(length2_ready, 1)
                    dve.wait_ge(length2_ready, q + 1)
                elif kind == "keys":
                    q = s[1]
                    js = slice((q % 2) * QT_, (q % 2 + 1) * QT_)
                    k4 = qkvb[:, js, C:2 * C].rearrange("p j (h e) -> p j h e", h=H)
                    dve.wait_ge(roots_ready, q + 1)
                    link(dve.tensor_scalar(kn[:, 1, :, :], kn[:, 1, :, :], TINY, None, ALU.max))
                    link(dve.reciprocal(kn[:, 2, :, :], kn[:, 1, :, :]))
                    link(dve.tensor_tensor(kn[:, 2, :, :], kn[:, 2, :, :], kn[:, 0, :, :], ALU.mult))
                    link(dve.tensor_tensor(kn[:, 2, :, :], kn[:, 2, :, :], kn[:, 1, :, :], ALU.add))
                    link(dve.tensor_scalar(kn[:, 2, :, :], kn[:, 2, :, :], 0.5, 1e-6, ALU.mult, ALU.add))
                    link(dve.reciprocal(kn[:, 2, :, :], kn[:, 2, :, :]))

                    def over_row(a):
                        return a.rearrange("p j (h o) -> p j h o", o=1).to_broadcast([P, QT_, H, D])

                    link(dve.tensor_tensor(k4, k4, over_row(kn[:, 2, :, :]), ALU.mult))
                    link(dve.tensor_scalar(kn[:, 0, :, :], beta[:, :, :], -1.0, None, ALU.mult))
                    dve.tensor_tensor(nkb[:, js, :].rearrange("p j (h e) -> p j h e", h=H), k4,
                                      over_row(kn[:, 0, :, :]), ALU.mult).then_inc(keys_ready, 1)
                    dve.wait_ge(keys_ready, q + 1)
                elif kind == "block":
                    b, j, part = s[1:]
                    m3 = M[:, :, :, :].rearrange("p r h e -> p r (h e)")
                    t3 = tmp[:, :, :, :].rearrange("p r h e -> p r (h e)")
                    if part == 0:
                        if j == 0:
                            link(dve.tensor_copy(dl[:, D:R, :],
                                                 qkvb[:, j, C:2 * C].rearrange("p (h d) -> p d h", h=H)))
                        else:
                            if j > 1:
                                dve.wait_ge(m_ready_pool, updates(b, j - 1))
                            k_j = qkvb[:, j, C:2 * C].rearrange("p (o c) -> p o c", o=1).to_broadcast([P, R, C])
                            link(dve.tensor_tensor(t3, m3, k_j, ALU.mult))
                    elif part == 1:
                        v_j = qkvb[:, j, 2 * C:3 * C].rearrange("p (h d) -> p d h", h=H)
                        if j == 0:
                            link(dve.tensor_scalar(dl[:, 0:D, :], v_j, -1.0, None, ALU.mult))
                        else:
                            link(dve.tensor_reduce(flat(dl[:, :, :]),
                                                   tmp[:, :, :, :].rearrange("p r h e -> p (r h) e"), AX_X, ALU.add))
                            dve.tensor_tensor(dl[:, 0:D, :], dl[:, 0:D, :], v_j, ALU.subtract)\
                               .then_inc(dl_ready, 1)
                            dve.wait_ge(dl_ready, updates(b, j))
                    elif part == 2:
                        if j == 0 and b:
                            dve.wait_ge(turn_full, 2 + turn_no["turn", "Q", b - 1, 1] + 1)
                        to, rows = (M, R) if j == 0 else (tmp, RV)
                        link(dve.tensor_tensor(to[:, 0:rows, :, :],
                                               dl[:, 0:rows, :].rearrange("p r (h o) -> p r h o", o=1)
                                               .to_broadcast([P, rows, H, D]),
                                               nkb[:, j, :].rearrange("p (o h e) -> p o h e", o=1, h=H)
                                               .to_broadcast([P, rows, H, D]), ALU.mult))
                    else:
                        n = b * BLK + j
                        if j:
                            dve.wait_ge(by_q_ready, n)
                            dve.tensor_reduce(flat(res[:, b, j - 1, :, :]),
                                              by_q[:, :, :, :].rearrange("p r h e -> p (r h) e"), AX_X,
                                              ALU.add).then_inc(res_ready, 1)
                            dve.wait_ge(res_ready, n)
                        if j == 0:
                            rows = M[:, D:R, :, :].rearrange("p r h e -> p (r h e)")
                            for e in range(D):
                                diag = rows[:, e * C + e:(e + 1) * C:D]
                                last = dve.tensor_scalar(diag, diag, 1.0, None, ALU.add)
                        elif j < BLK:
                            last = dve.tensor_tensor(m3[:, 0:RV, :], m3[:, 0:RV, :], t3[:, 0:RV, :], ALU.add)
                        if j < BLK:
                            last.then_inc(m_ready, 1)
                            dve.wait_ge(m_ready, n + 1)
                elif kind == "read":
                    b, j = s[1:]
                    if j == 0:
                        dve.wait_ge(turn_used, turned(("turn", "S", b, 1)))
                        if b:
                            dve.wait_ge(turn_full, 2 + turn_no["turn", "O", b - 1, 1] + 1)
                    o_j = O[:, j, :, :].rearrange("p h d -> p d h")
                    if by_pool(b, j):
                        t4 = s_by_q(j)
                        dve.wait_ge(s_by_q_ready, j // 2 + 1)
                    else:
                        t4 = by_back
                        link(dve.tensor_tensor(t4, S[:, :, :, :], back(b, j), ALU.mult))
                    link(dve.tensor_reduce(o_j, t4, AX_X, ALU.add))
                    dve.tensor_tensor(o_j, o_j, res[:, b, j, 0:D, :], ALU.add).then_inc(o_ready, 1)
                    dve.wait_ge(o_ready, read_no[s] + 1)


_INS = ["L0_attn_a_residual", "L0_attn_a_w_fc", "L0_attn_a_w_proj", "L0_attn_a_ln_g", "L0_attn_a_ln_b",
        "L0_attn_b_Wq", "L0_attn_b_bq", "L0_attn_b_Wk", "L0_attn_b_bk", "L0_attn_b_Wv", "L0_attn_b_bv",
        "L0_attn_b_Wbeta", "L0_attn_b_bbeta", "L0_attn_b_Wo", "L0_attn_b_bo",
        "L0_ffn_W1", "L0_ffn_b1", "L0_ffn_W2", "L0_ffn_b2"]


def kernel(**inputs):
    import numpy as _np
    import concourse.bacc as _bacc
    from concourse import mybir as _mybir
    from concourse.bass_utils import run_bass_kernel_spmd as _run

    nc = _bacc.Bacc("TRN2", target_bir_lowering=False, num_devices=1)
    arrays, args = {}, []
    for name in _INS:
        a = _np.ascontiguousarray(inputs[name])
        arrays[f"in_{name}"] = a
        args.append(nc.dram_tensor(f"in_{name}", a.shape, _mybir.dt.from_np(a.dtype), kind="ExternalInput").ap())
    shape = inputs["L0_attn_a_residual"].shape
    args.append(nc.dram_tensor("out_0", shape, _mybir.dt.float32, kind="ExternalOutput").ap())
    layer_kernel(nc, *args)
    r = _run(nc, [arrays], core_ids=[0])
    return r.results[0]["out_0"]
```
